# Optimizing a Trainium2 kernel written in Bass

```python
import numpy as np
import jax
import jax.numpy as jnp

def _softmax(x, axis=-1):
    return jax.nn.softmax(x, axis=axis)

def _gelu(x):
    return jax.nn.gelu(x, approximate=True)

def _silu(x):
    return jax.nn.silu(x)

def _sigmoid(x):
    return jax.nn.sigmoid(x)

def _layernorm(x, axis=-1, eps=1e-05):
    m = jnp.mean(x, axis=axis, keepdims=True)
    v = jnp.var(x, axis=axis, keepdims=True)
    return (x - m) / jnp.sqrt(v + eps)

def _scatter_add(tgt, idx, src, axis=0):
    return tgt.at[idx].add(src)

def _segment_sum(src, seg, n):
    return jax.ops.segment_sum(src, seg, n)
kernel_name = 'mk_xattn_seq_d1_seqx_r4_086c36'

def setup_inputs(seed: int=0):
    np.random.seed(seed)
    _w = jnp.asarray

    def _rec_inputs():
        import jax
        import jax.numpy as jnp
        _rk = jax.random.key(seed)
        x = -0.0002928 + 1 * jax.random.normal(jax.random.fold_in(_rk, 1), (8, 256, 256), jnp.float32)
        _lenS = 256 - jax.random.randint(jax.random.fold_in(_rk, 7), (8,), 0, max(1, 256 // 4) + 1, jnp.int32)
        _lenS2 = 77 - jax.random.randint(jax.random.fold_in(_rk, 8), (8,), 0, max(1, 77 // 4) + 1, jnp.int32)
        _ctx_1024P = jax.random.normal(jax.random.fold_in(_rk, 11), (8, 16, 256), jnp.float32)
        _ctx_1024c = jax.random.dirichlet(jax.random.fold_in(_rk, 511), 0.3 * jnp.ones((16,), jnp.float32), (8, 77))
        _ctx_1024t = jnp.einsum('bsk,bkd->bsd', _ctx_1024c, _ctx_1024P)
        _ctx_1024t = _ctx_1024t * jax.lax.rsqrt(jnp.mean(jnp.square(_ctx_1024t)) + 1e-12) * 0.953939
        ctx_1024 = 4.13588e-05 + 0.999923 * (_ctx_1024t + 0.3 * jax.random.normal(jax.random.fold_in(_rk, 611), (8, 77, 256), jnp.float32))
        return (x, ctx_1024)
    x, ctx_1024 = _rec_inputs()

    def _L0_xattn_setup():
        import jax, jax.numpy as jnp
        import numpy as np
        E = 256
        H = 16
        HD = E // H
        EPS = 1e-05

        def _layer_norm(x, g, b):
            mu = jnp.mean(x, axis=-1, keepdims=True)
            var = jnp.var(x, axis=-1, keepdims=True)
            return (x - mu) * jax.lax.rsqrt(var + EPS) * g + b
        key = jax.random.key(seed)
        ks = jax.random.split(key, 16)
        s = 0.02
        inp = {'query': jax.random.normal(ks[0], (4, 256, E), jnp.float32), 'key': jax.random.normal(ks[1], (4, 512, E), jnp.float32), 'value': jax.random.normal(ks[2], (4, 512, E), jnp.float32), 'wq': jax.random.normal(ks[3], (E, E), jnp.float32) * s, 'bq': jnp.zeros((E,), jnp.float32), 'wk': jax.random.normal(ks[4], (E, E), jnp.float32) * s, 'bk': jnp.zeros((E,), jnp.float32), 'wv': jax.random.normal(ks[5], (E, E), jnp.float32) * s, 'bv': jnp.zeros((E,), jnp.float32), 'wo': jax.random.normal(ks[6], (E, E), jnp.float32) * s, 'bo': jnp.zeros((E,), jnp.float32), 'ln1_g': jnp.ones((E,), jnp.float32), 'ln1_b': jnp.zeros((E,), jnp.float32), 'ln2_g': jnp.ones((E,), jnp.float32), 'ln2_b': jnp.zeros((E,), jnp.float32), 'w1': jax.random.normal(ks[7], (E, 4 * E), jnp.float32) * s, 'b1': jnp.zeros((4 * E,), jnp.float32), 'w2': jax.random.normal(ks[8], (4 * E, E), jnp.float32) * s, 'b2': jnp.zeros((E,), jnp.float32)}
        return inp
    _L0_xattn_all = _L0_xattn_setup()
    _L0_xattn_in = {k: v for k, v in _L0_xattn_all.items() if k in ('wq', 'bq', 'wk', 'bk', 'wv', 'bv', 'wo', 'bo', 'ln1_g', 'ln1_b', 'ln2_g', 'ln2_b', 'w1', 'b1', 'w2', 'b2')}
    del _L0_xattn_all
    return {'x': x, 'ctx_1024': ctx_1024, 'L0_xattn_wq': _L0_xattn_in['wq'], 'L0_xattn_bq': _L0_xattn_in['bq'], 'L0_xattn_wk': _L0_xattn_in['wk'], 'L0_xattn_bk': _L0_xattn_in['bk'], 'L0_xattn_wv': _L0_xattn_in['wv'], 'L0_xattn_bv': _L0_xattn_in['bv'], 'L0_xattn_wo': _L0_xattn_in['wo'], 'L0_xattn_bo': _L0_xattn_in['bo'], 'L0_xattn_ln1_g': _L0_xattn_in['ln1_g'], 'L0_xattn_ln1_b': _L0_xattn_in['ln1_b'], 'L0_xattn_ln2_g': _L0_xattn_in['ln2_g'], 'L0_xattn_ln2_b': _L0_xattn_in['ln2_b'], 'L0_xattn_w1': _L0_xattn_in['w1'], 'L0_xattn_b1': _L0_xattn_in['b1'], 'L0_xattn_w2': _L0_xattn_in['w2'], 'L0_xattn_b2': _L0_xattn_in['b2']}

def reference(x, ctx_1024, L0_xattn_wq, L0_xattn_bq, L0_xattn_wk, L0_xattn_bk, L0_xattn_wv, L0_xattn_bv, L0_xattn_wo, L0_xattn_bo, L0_xattn_ln1_g, L0_xattn_ln1_b, L0_xattn_ln2_g, L0_xattn_ln2_b, L0_xattn_w1, L0_xattn_b1, L0_xattn_w2, L0_xattn_b2):
    import jax
    import jax.numpy as jnp

    def _L0_xattn_ref(query, key, value, wq, bq, wk, bk, wv, bv, wo, bo, ln1_g, ln1_b, ln2_g, ln2_b, w1, b1, w2, b2):
        import jax, jax.numpy as jnp
        import numpy as np
        E = 256
        H = 16
        HD = E // H
        EPS = 1e-05

        def _layer_norm(x, g, b):
            mu = jnp.mean(x, axis=-1, keepdims=True)
            var = jnp.var(x, axis=-1, keepdims=True)
            return (x - mu) * jax.lax.rsqrt(var + EPS) * g + b
        B, Sq, _ = query.shape
        Sk = key.shape[1]
        residual = query
        qn = _layer_norm(query, ln1_g, ln1_b)
        kn = _layer_norm(key, ln1_g, ln1_b)
        vn = _layer_norm(value, ln1_g, ln1_b)
        Q = (qn @ wq + bq).reshape(B, Sq, H, HD)
        K = (kn @ wk + bk).reshape(B, Sk, H, HD)
        V = (vn @ wv + bv).reshape(B, Sk, H, HD)
        scores = jnp.einsum('bqhd,bkhd->bhqk', Q, K) / jnp.sqrt(jnp.float32(HD))
        attn = jax.nn.softmax(scores, axis=-1)
        out = jnp.einsum('bhqk,bkhd->bqhd', attn, V).reshape(B, Sq, E)
        out = out @ wo + bo
        x = residual + out
        residual2 = x
        y = _layer_norm(x, ln2_g, ln2_b)
        y = jax.nn.gelu(y @ w1 + b1, approximate=False)
        y = y @ w2 + b2
        return residual2 + y
    x = _L0_xattn_ref(x, ctx_1024, ctx_1024, L0_xattn_wq, L0_xattn_bq, L0_xattn_wk, L0_xattn_bk, L0_xattn_wv, L0_xattn_bv, L0_xattn_wo, L0_xattn_bo, L0_xattn_ln1_g, L0_xattn_ln1_b, L0_xattn_ln2_g, L0_xattn_ln2_b, L0_xattn_w1, L0_xattn_b1, L0_xattn_w2, L0_xattn_b2)
    return x

_drawn_inputs = setup_inputs


def setup_inputs(seed=0):
    import zlib

    import numpy as np

    out = dict(_drawn_inputs(seed))
    spreads = {'L0_xattn_bq': (0.0, 0.8),
     'L0_xattn_bk': (0.0, 0.8),
     'L0_xattn_bv': (0.0, 0.1),
     'L0_xattn_bo': (0.0, 0.1),
     'L0_xattn_ln1_g': (1.0, 0.6),
     'L0_xattn_ln1_b': (0.0, 0.775),
     'L0_xattn_ln2_g': (1.0, 0.6),
     'L0_xattn_ln2_b': (0.0, 0.673),
     'L0_xattn_b1': (0.0, 0.1),
     'L0_xattn_b2': (0.0, 0.1)}
    factors = {'L0_xattn_wq': 8.0, 'L0_xattn_wk': 8.0}
    for name, (base, spread) in spreads.items():
        noise = np.random.default_rng([zlib.crc32(name.encode()), seed]).standard_normal(out[name].shape)
        drawn = base * np.exp(spread * noise) if base else spread * noise
        out[name] = jnp.asarray(drawn.astype(out[name].dtype))
    for name, factor in factors.items():
        out[name] = (out[name] * factor).astype(out[name].dtype)
    return out
```

```python
import concourse.bass as bass
from concourse import mybir
from contextlib import ExitStack



def xattn_block_kernel(nc, x, ctx_in, wq, wk, wv, wo, w1, w2, columns, rows, out):
    f32, f16, i32 = mybir.dt.float32, mybir.dt.float16, mybir.dt.int32
    ALU, ACT, AX = mybir.AluOpType, mybir.ActivationFunctionType, mybir.AxisListType

    NBATCH, SQ, E = x.shape
    SK = ctx_in.shape[1]
    F = w1.shape[1]
    H = 16
    HD = E // H
    P = 128
    KT = E // P
    MT = F // P
    PAIRS = NBATCH // 2
    TOK = 2 * SQ
    TT = TOK // P
    NTOK = NBATCH * SQ
    CTOK = NBATCH * SK
    CSTART = [0, 128, 256, 384, CTOK - P]
    CTT = len(CSTART)
    CCH = CTOK // 2
    SK2 = 2 * SK
    NG = H // 2
    FILLS = [(0, 1, 2), (3, 4, 5), (6, 7)]
    NF = len(FILLS) * TT
    EPS = 1e-5
    SEL = 32768.0
    RSQRT_SEED = float(0x5F3759DF)
    NEWTON = 3

    def head_of(slot):
        pos = slot // 2
        return 2 * ((pos % 2) * 4 + pos // 2) + slot % 2

    x_t = x.rearrange("b s e -> (b s) e").rearrange("(t p) e -> p t e", p=P)
    out_t = out.rearrange("b s e -> (b s) e").rearrange("(t p) e -> p t e", p=P)
    ctx_rows = ctx_in.rearrange("b s e -> (b s) e")

    stack = ExitStack()
    with stack:
        def sb(name, shape, dt):
            return stack.enter_context(nc.sbuf_tensor(name, shape, dt))

        def sem(name):
            return stack.enter_context(nc.semaphore(name))

        x_sb = sb("x_sb", [P, NTOK // P, E], f32)
        shared = sb("shared", [P, H * TOK], f32)
        shared_g = sb("shared_g", [P, MT * TOK], f32)
        taken = [0]

        def in_shared(dt, words, pattern, **dims):
            view = shared[:, taken[0]:taken[0] + words]
            taken[0] += words
            return (view.bitcast(dt) if dt != f32 else view).rearrange(pattern, **dims)

        c_sb = in_shared(f32, CTT * E, "p (t e) -> p t e", e=E)
        wraw = {n: in_shared(f32, KT * E, "p (c n) -> p c n", n=E) for n in ("q", "k", "v")}
        wraw["o"] = sb("raw_o", [P, KT, E], f32)
        wraw["1"] = shared_g[:, 0:KT * F].rearrange("p (c n) -> p c n", n=F)
        wraw["2"] = shared_g[:, KT * F:KT * F + MT * E].rearrange("p (c n) -> p c n", n=E)
        wp = {n: sb(f"parts_{n}", [P, 2] + list(wraw[n].shape[1:]), f16) for n in wraw}
        cols = sb("cols", [P, 6 * KT + MT], f32)
        lng = {1: cols[:, 0:KT], 2: cols[:, 2 * KT:3 * KT]}
        lnb = {1: cols[:, KT:2 * KT], 2: cols[:, 3 * KT:4 * KT]}
        bcol = {"q": cols[:, 4 * KT:5 * KT], "k": cols[:, 5 * KT:6 * KT], "1": cols[:, 6 * KT:6 * KT + MT]}
        brows = sb("brows", [P, 3, E], f32)
        brow = {n: brows[:, j, :] for j, n in enumerate(("v", "o", "2"))}
        lnb1_rep = in_shared(f32, KT * P, "p (c n) -> p c n", n=P)
        bfull = {n: sb(f"bfull_{n}", [P, MT if n == "1" else KT], f32) for n in bcol}
        bscaled = {n: sb(f"bscaled_{n}", [P, KT], f32) for n in ("q", "k")}
        bv_full = sb("bv_full", [P, E], f32)
        bv_scaled = sb("bv_scaled", [P, E], f32)
        amax = {"a": sb("amax_a", [P, 6], f32), "b": sb("amax_b", [P, 4], f32)}
        amax_all = {"a": sb("amax_all_a", [P, 6], f32), "b": sb("amax_all_b", [P, 4], f32)}
        mag = sb("mag", [P, 6], f32)
        pow2 = sb("pow2", [P, 6], f32)
        inv = sb("inv", [P, 6], f32)
        scale_up = sb("scale_up", [P, 6], f32)
        scale_dn = sb("scale_dn", [P, 6], f32)
        sc_exp0 = sb("sc_exp0", [P, 1], f32)
        sc_exp = sb("sc_exp", [P, 1], f32)
        sc_vo = sb("sc_vo", [P, 1], f32)
        sc_12 = sb("sc_12", [P, 1], f32)
        COL = {"q": 0, "k": 1, "v": 2, "1": 3, "o": 4, "2": 5}

        ident16 = sb("ident16", [P, P], f16)
        ident32 = sb("ident32", [P, P], f32)
        blocks = sb("blocks", [P, 8], f32)
        evenodd = sb("evenodd", [P, 2], f32)
        selector = sb("selector", [P, H], f16)

        c_hat = in_shared(f32, CTT * E, "p (t e) -> p t e", e=E)
        c_parts = in_shared(f16, CTT * E, "p (a t e) -> p a t e", a=2, e=E)
        cT = in_shared(f16, KT * CTOK, "p (a k n) -> p a k n", a=2, k=KT)
        k_hi = in_shared(f16, KT * CTOK // 2, "p (k n) -> p k n", k=KT)
        k_lo = in_shared(f16, KT * CTOK // 2, "p (k n) -> p k n", k=KT)
        kpack = sb("kpack", [96, H, CTOK], f16)
        v_all = sb("v_all", [SK, NBATCH, E], f32)
        k_cur = sb("k_cur", [P, H, SK2], f16)
        v_cur = sb("v_cur", [SK, 2, H, 32], f32)
        x_hat = sb("x_hat", [P, TT, E], f32)
        x_parts = sb("x_parts", [P, 2, TT, E], f16)
        xT = sb("xT", [P, 2, KT, TOK], f16)
        q_hi = sb("q_hi", [P, KT, TOK], f16)
        q_lo = sb("q_lo", [P, KT, TOK], f16)
        qpack = sb("qpack", [P, NG, TOK], f16)
        smax = sb("smax", [P, TT, H], f32)
        m_parts = sb("m_parts", [P, TT, 2, H], f16)
        mT = sb("mT", [P, TOK], f16)
        probs = shared[0:SK, :].rearrange("p (h n) -> p h n", h=H)
        oT = sb("oT", [P, 4, TOK], f32)
        rden = sb("rden", [P, TT, H], f32)
        o_nat = sb("o_nat", [P, TT, E], f32)
        o_parts = sb("o_parts", [P, 2, TT, E], f16)
        onT = sb("onT", [P, 2, KT, TOK], f16)
        x_res = sb("x_res", [P, TT, E], f32)
        x1 = sb("x1", [P, TT, E], f32)
        x1_res = sb("x1_res", [P, TT, E], f32)
        y_hat = sb("y_hat", [P, TT, E], f32)
        y_parts = sb("y_parts", [P, 2, TT, E], f16)
        yT = sb("yT", [P, 2, KT, TOK], f16)
        g_full = sb("g_full", [P, 2, TOK], f32)
        g_parts = shared_g[:, :].bitcast(f16).rearrange("p (a m n) -> p a m n", a=2, m=MT)
        g_hi, g_lo = g_parts[:, 0], g_parts[:, 1]
        ln_buf = {n: dict(st=sb(f"ln{n}_st", [P, w, 6], f32), mean=sb(f"ln{n}_mean", [P, w], f32),
                          v=sb(f"ln{n}_v", [P, w], f32), h=sb(f"ln{n}_h", [P, w], f32),
                          a=sb(f"ln{n}_a", [P, w], f32), b=sb(f"ln{n}_b", [P, w], f32),
                          c=sb(f"ln{n}_c", [P, w], f32), y=sb(f"ln{n}_y", [P, w], f32))
                  for n, w in (("c", CTT), ("1", TT), ("2", TT))}

        bank = stack.enter_context(nc.psum_tensor("bank", [P, 8, 512], f32))

        def half16(b):
            return bank[:, b, :].bitcast(f16)

        ld_c = [sem(f"ld_c{i}") for i in range(2)]
        ld_x = [sem(f"ld_x{i}") for i in range(PAIRS)]
        ld_w = {n: sem(f"ld_w{n}") for n in wraw}
        ld_cols, ld_rows = sem("ld_cols"), sem("ld_rows")
        pool_const = sem("pool_const")
        consts_ready = sem("consts_ready")
        lnb_rep_ready = sem("lnb_rep_ready")
        ln_step = {n: sem(f"ln_step_{n}") for n in ("c", "1", "2")}
        hat_ready = {n: sem(f"hat_ready_{n}") for n in ("c", "1", "2")}
        hi_ready = {n: sem(f"hi_ready_{n}") for n in ("c", "1", "2", "o")}
        lo_ready = {n: sem(f"lo_ready_{n}") for n in ("c", "1", "2", "o")}
        cT_done, cT_hi, cT_lo = sem("cT_done"), sem("cT_hi"), sem("cT_lo")
        bias_mm = {"a": sem("bias_mm_a"), "b": sem("bias_mm_b")}
        gained = {"a": sem("gained_a_ready"), "b": sem("gained_b_ready")}
        amax_ready = {"a": sem("amax_ready_a"), "b": sem("amax_ready_b")}
        amax_shared = {"a": sem("amax_shared_a"), "b": sem("amax_shared_b")}
        scale_step = {"a": sem("scale_step_a"), "b": sem("scale_step_b")}
        scales_ready = {"a": sem("scales_ready_a"), "b": sem("scales_ready_b")}
        whi_ready = {n: sem(f"whi_{n}") for n in wraw}
        wlo_ready = {n: sem(f"wlo_{n}") for n in wraw}
        k_mm, khi_ready, klo_ready = sem("k_mm"), sem("khi_ready"), sem("klo_ready")
        kpack_loaded, kpack_masked = sem("kpack_loaded"), sem("kpack_masked")
        v_mm, v_ready = sem("v_mm"), sem("v_ready")
        kcur_ready, vcur_ready = sem("kcur_ready"), sem("vcur_ready")
        xres_ready, x1res_ready = sem("xres_ready"), sem("x1res_ready")
        xT_done, xT_hi, xT_lo = sem("xT_done"), sem("xT_hi"), sem("xT_lo")
        q_done, qhi_ready, qlo_ready = sem("q_done"), sem("qhi_ready"), sem("qlo_ready")
        qpack_ready = sem("qpack_ready")
        s_done, smax_ready = sem("s_done"), sem("smax_ready")
        mhi_ready, m_ready, mT_done, mT_copied, m_rows = [sem(n) for n in (
            "mhi_ready", "m_ready", "mT_done", "mT_copied", "m_rows")]
        st_done, exp_done = sem("st_done"), sem("exp_done")
        pv_done, oT_ready = sem("pv_done"), sem("oT_ready")
        on_done, rden_ready, onat_ready = sem("on_done"), sem("rden_ready"), sem("onat_ready")
        onT_done, onT_hi, onT_lo = sem("onT_done"), sem("onT_hi"), sem("onT_lo")
        wo_done, x1_ready = sem("wo_done"), sem("x1_ready")
        yT_done, yT_hi, yT_lo = sem("yT_done"), sem("yT_hi"), sem("yT_lo")
        f1_done, gelu_done, ghi_ready, glo_ready = [sem(n) for n in ("f1_done", "gelu_done", "ghi_ready", "glo_ready")]
        f2_done, out_ready, out_stored = sem("f2_done"), sem("out_ready"), sem("out_stored")

        block = stack.enter_context(nc.Block())

        def wait(eng, s, value):
            if isinstance(value, int) and value <= 0:
                return
            eng.wait_ge(s, value)

        @block.sync
        def _(sp):
            for i, (lo, hi) in enumerate(((0, 4), (4, 5))):
                src = ctx_rows[0:4 * P, :].rearrange("(t p) e -> p t e", p=P) if i == 0 else \
                    ctx_rows[CTOK - P:CTOK, :].rearrange("(t p) e -> p t e", p=P)
                sp.dma_start(c_sb[:, lo:hi, :], src).then_inc(ld_c[i], 16)
            for n, w in (("k", wk), ("v", wv), ("q", wq)):
                sp.dma_start(wraw[n][:, :, :], w.rearrange("(c p) n -> p c n", p=P)).then_inc(ld_w[n], 16)
            sp.dma_start(x_sb[:, 0:TT, :], x_t[:, 0:TT, :]).then_inc(ld_x[0], 16)
            for hh in range(2):
                for c1 in range(2):
                    src = wo.rearrange("(c k h r) n -> c h r k n", c=2, k=2, h=2)[c1, hh]
                    at = hh * 64 + c1 * 32
                    sp.dma_start(wraw["o"][at:at + 32, :, :], src).then_inc(ld_w["o"], 16)
            sp.dma_start(wraw["1"][:, :, :], w1.rearrange("(c p) n -> p c n", p=P)).then_inc(ld_w["1"], 16)
            sp.dma_start(wraw["2"][:, :, :], w2.rearrange("(c p) n -> p c n", p=P)).then_inc(ld_w["2"], 16)

            for part, src in ((0, k_hi), (1, k_lo)):
                for j in range(4):
                    sp.wait_ge(khi_ready, 2 * KT) if part == 0 else sp.wait_ge(klo_ready, 2 * KT)
                    for role in ((0, 1) if part == 0 else (2,)):
                        for u in range(2):
                            dst = kpack[32 * role:32 * role + 32, 4 * j + u:4 * j + u + 3:2, :]
                            sp.dma_start(dst, src[32 * j:32 * j + 32, :, :]).then_inc(kpack_loaded, 16)
            for i in range(1, PAIRS):
                sp.dma_start(x_sb[:, i * TT:(i + 1) * TT, :], x_t[:, i * TT:(i + 1) * TT, :]).then_inc(ld_x[i], 16)

            def pack_q(a):
                wait(sp, st_done, a * NG)
                for part, src in ((0, q_hi), (1, q_lo)):
                    sp.wait_ge((qhi_ready, qlo_ready)[part], a * KT + KT)
                    for role in ((0, 2) if part == 0 else (1,)):
                        for j in range(4):
                            sp.dma_start(qpack[32 * role:32 * role + 32, 2 * j:2 * j + 2, :],
                                         src[32 * j:32 * j + 32, :, :]).then_inc(qpack_ready, 16)

            def store(f):
                for t in range(TT):
                    sp.wait_ge(out_ready, f * TT + t + 1)
                    sp.dma_start(out_t[:, bass.ds(f * TT + t, 1), :], x1_res[:, t:t + 1, :]).then_inc(out_stored, 16)

            pack_q(0)
            with sp.Fori(0, PAIRS - 1) as i:
                pack_q(i + 1)
                store(i)
            store(PAIRS - 1)
            sp.wait_ge(out_stored, 16 * TT * PAIRS)

        @block.gpsimd
        def _(pool):
            made = [0]

            def const_step(ins):
                made[0] += 1
                ins.then_inc(pool_const, 1)
                pool.wait_ge(pool_const, made[0])

            for m in (ident16, ident32):
                const_step(pool.memset(m[:, :], 0.0))
                const_step(pool.affine_select(out=m[:, :], in_=m[:, :], compare_op=ALU.not_equal, fill=1.0, base=0,
                                              pattern=[[-1, P]], channel_multiplier=1))
            const_step(pool.memset(blocks[:, :], 1.0))
            const_step(pool.affine_select(out=blocks[:, :], in_=blocks[:, :], compare_op=ALU.is_ge, fill=0.0,
                                          base=0, pattern=[[-16, 8]], channel_multiplier=1))
            const_step(pool.affine_select(out=blocks[:, :], in_=blocks[:, :], compare_op=ALU.is_ge, fill=0.0,
                                          base=15, pattern=[[16, 8]], channel_multiplier=-1))
            const_step(pool.memset(selector[96:128, :], 0.0))
            for first in (0, 16):
                const_step(pool.affine_select(out=selector[96:128, :], in_=selector[96:128, :],
                                              compare_op=ALU.not_equal, fill=SEL, base=-first,
                                              pattern=[[-1, H]], channel_multiplier=1))
            const_step(pool.memset(v_cur[:, :, :, :], 0.0))
            const_step(pool.memset(v_cur[:, :, :, HD:HD + 1], 1.0))
            for g in ("a", "b"):
                pool.wait_ge(amax_ready[g], 6 if g == "a" else 4)
                pool.partition_all_reduce(amax_all[g][:, :], amax[g][:, :], P,
                                          bass.bass_isa.ReduceOp.max).then_inc(amax_shared[g], 1)
                pool.wait_ge(amax_shared[g], 1)

            def copy_kv(a):
                wait(pool, st_done, a * NG)
                pool.tensor_copy(k_cur[0:96, :, :].bitcast(i32),
                                 kpack[:, :, bass.ds(a * SK2, SK2)].bitcast(i32)).then_inc(kcur_ready, 1)
                pool.wait_ge(kcur_ready, a + 1)
                wait(pool, pv_done, a * 4)
                pool.tensor_copy(v_cur[:, :, :, 0:HD],
                                 v_all[:, bass.ds(2 * a, 2), :].rearrange("p b (h d) -> p b h d", h=H))\
                    .then_inc(vcur_ready, 1)
                pool.wait_ge(vcur_ready, a + 1)
                wait(pool, x1_ready, a * TT)
                pool.tensor_tensor(x_res[:, :, :], x_sb[:, bass.ds(a * TT, TT), :],
                                   brow["o"][:, None, :].broadcast_to([P, TT, E]), ALU.add).then_inc(xres_ready, 1)
                pool.wait_ge(xres_ready, a + 1)

            def x1_with_bias(a):
                pool.wait_ge(x1_ready, a * TT + TT)
                wait(pool, out_stored, a * TT * 16)
                pool.tensor_tensor(x1_res[:, :, :], x1[:, :, :],
                                   brow["2"][:, None, :].broadcast_to([P, TT, E]), ALU.add).then_inc(x1res_ready, 1)
                pool.wait_ge(x1res_ready, a + 1)

            pool.wait_ge(kpack_masked, 2)
            pool.wait_ge(v_ready, NBATCH // 2)
            pool.wait_ge(ld_rows, 16)
            for i in range(PAIRS):
                pool.wait_ge(ld_x[i], 16)
            copy_kv(0)
            x1_with_bias(0)
            with pool.Fori(0, PAIRS - 1) as i:
                copy_kv(i + 1)
                x1_with_bias(i + 1)

        @block.scalar
        def _(act):
            def hi_part(n, a, src, dst):
                act.wait_ge(hat_ready[n], a + 1)
                act.activation(dst[:, 0], src[:, :, :], ACT.Copy).then_inc(hi_ready[n], 1)

            act.dma_start(cols[:, :], columns).then_inc(ld_cols, 16)
            act.dma_start(brows[:, :, :], rows.partition_broadcast(P)).then_inc(ld_rows, 16)
            act.wait_ge(pool_const, 12)
            act.activation(k_cur[96:128, :, :], selector[96:128, :, None].broadcast_to([32, H, SK2]),
                           ACT.Copy).then_inc(consts_ready, 1)
            hi_part("c", 0, c_hat, c_parts)
            for n in ("k", "v", "q"):
                if n == "k":
                    act.wait_ge(scales_ready["a"], 1)
                    act.wait_ge(gained["a"], 2 * KT + KT)
                act.activation(wp[n][:, 0], wraw[n][:, :, :], ACT.Copy, scale=scale_up[:, COL[n]:COL[n] + 1])\
                    .then_inc(whi_ready[n], 1)
            for t in range(CTT):
                act.wait_ge(cT_done, t + 1)
                act.activation(cT[:, 0, :, t * P:CSTART[t] + P],
                               half16(t % 4)[:, 0:2 * P].rearrange("p (k n) -> p k n", k=KT)
                               [:, :, t * P - CSTART[t]:], ACT.Copy)\
                    .then_inc(cT_hi, 1)
            for h in range(KT):
                for c in range(2):
                    act.wait_ge(k_mm, 2 * h + c + 1)
                    act.activation(k_hi[:, h, c * CCH:(c + 1) * CCH], bank[:, 4 + 2 * h + c, 0:CCH], ACT.Identity,
                                   bias=bscaled["k"][:, h:h + 1]).then_inc(khi_ready, 1)

            def attention_front(a):
                act.wait_ge(xT_done, 2 * a + 1)
                act.activation(xT[:, 0, :, :], half16(0).rearrange("p (k n) -> p k n", k=KT), ACT.Copy)\
                    .then_inc(xT_hi, 1)
                wait(act, qpack_ready, a * 12 * 16)
                for h in range(KT):
                    act.wait_ge(q_done, a * KT + h + 1)
                    act.activation(q_hi[:, h, :], bank[:, 2 + h, :], ACT.Identity, bias=bscaled["q"][:, h:h + 1])\
                        .then_inc(qhi_ready, 1)

            def weights_b():
                act.wait_ge(scales_ready["b"], 1)
                act.wait_ge(gained["b"], KT)
                for n, src in (("o", wraw["o"]), ("1", wraw["1"]), ("2", wraw["2"])):
                    act.activation(wp[n][:, 0], src[:, :, :], ACT.Copy, scale=scale_up[:, COL[n]:COL[n] + 1])\
                        .then_inc(whi_ready[n], 1)

            def softmax(a):
                wait(act, pv_done, 4 * a)
                for s in range(NG):
                    act.wait_ge(st_done, a * NG + s + 1)
                    b0 = 2 * (s % 2)
                    act.activation(probs[:, 2 * s:2 * s + 2, :], bank[0:SK, b0:b0 + 2, :], ACT.Exp,
                                   scale=sc_exp[0:SK, :]).then_inc(exp_done, 1)

            def attention_back(a):
                wait(act, on_done, 4 * a)
                for g in range(4):
                    act.wait_ge(pv_done, 4 * a + g + 1)
                    act.activation(oT[:, g, :], bank[:, 4 + g % 2, :], ACT.Copy).then_inc(oT_ready, 1)
                act.wait_ge(onat_ready, TT * (a + 1))
                wait(act, onT_done, 2 * a)
                act.activation(o_parts[:, 0], o_nat[:, :, :], ACT.Copy).then_inc(hi_ready["o"], 1)
                act.wait_ge(onT_done, 2 * a + 1)
                wait(act, wo_done, TT * a)
                act.activation(onT[:, 0, :, :], half16(4).rearrange("p (k n) -> p k n", k=KT), ACT.Copy)\
                    .then_inc(onT_hi, 1)
                hi_part("2", a, y_hat, y_parts)

            def mlp_front(f):
                act.wait_ge(yT_done, 2 * f + 1)
                act.activation(yT[:, 0, :, :], half16(4).rearrange("p (k n) -> p k n", k=KT), ACT.Copy)\
                    .then_inc(yT_hi, 1)

            def gelus(f, m0, m1):
                for m in range(m0, m1):
                    act.wait_ge(f1_done, f * MT + m + 1)
                    if m >= 2:
                        act.wait_ge(glo_ready, f * MT + m - 1)
                    act.activation(g_full[:, m % 2, :], bank[:, 6 + m % 2, :], ACT.Gelu,
                                   bias=bfull["1"][:, m:m + 1], scale=scale_dn[:, 3:4]).then_inc(gelu_done, 1)
                    act.wait_ge(gelu_done, f * MT + m + 1)
                    act.activation(g_hi[:, m, :], g_full[:, m % 2, :], ACT.Copy, scale=scale_up[:, 3:4])\
                        .then_inc(ghi_ready, 1)

            hi_part("1", 0, x_hat, x_parts)
            attention_front(0)
            weights_b()
            softmax(0)
            hi_part("1", 1, x_hat, x_parts)
            attention_back(0)

            def both(i, last=False):
                attention_front(i + 1)
                mlp_front(i)
                gelus(i, 0, MT)
                softmax(i + 1)
                if not last:
                    hi_part("1", i + 2, x_hat, x_parts)
                attention_back(i + 1)

            with act.Fori(0, PAIRS - 2) as i:
                both(i)
            both(PAIRS - 2, last=True)
            mlp_front(PAIRS - 1)
            gelus(PAIRS - 1, 0, MT)

        @block.vector
        def _(dve):
            def layer_norm(n, a, src, tiles, hat):
                b = ln_buf[n]
                steps = tiles + 9 + 4 * NEWTON
                at = a * steps
                k = 0
                for t in range(tiles):
                    dve.bn_stats(b["st"][:, t, :], src(t)).then_inc(ln_step[n], 1)
                k += tiles
                dve.wait_ge(ln_step[n], at + k)
                mean_e, mean_o = b["st"][:, :, 1], b["st"][:, :, 4]
                dve.tensor_tensor(b["a"][:, :], mean_e, mean_o, ALU.add).then_inc(ln_step[n], 1)
                dve.tensor_tensor(b["b"][:, :], mean_e, mean_o, ALU.subtract).then_inc(ln_step[n], 1)
                dve.tensor_tensor(b["c"][:, :], b["st"][:, :, 2], b["st"][:, :, 5], ALU.add).then_inc(ln_step[n], 1)
                k += 3
                dve.wait_ge(ln_step[n], at + k)
                dve.tensor_scalar(b["mean"][:, :], b["a"][:, :], 0.5, None, ALU.mult).then_inc(ln_step[n], 1)
                dve.tensor_tensor(b["h"][:, :], b["b"][:, :], b["b"][:, :], ALU.mult).then_inc(ln_step[n], 1)
                dve.tensor_scalar(b["y"][:, :], b["c"][:, :], 1.0 / E, EPS, ALU.mult, ALU.add)\
                    .then_inc(ln_step[n], 1)
                k += 3
                dve.wait_ge(ln_step[n], at + k)
                dve.scalar_tensor_tensor(b["v"][:, :], b["h"][:, :], 0.25, b["y"][:, :], ALU.mult, ALU.add)\
                    .then_inc(ln_step[n], 1)
                k += 1
                dve.wait_ge(ln_step[n], at + k)
                dve.tensor_scalar(b["h"][:, :].bitcast(i32), b["v"][:, :].bitcast(i32), 1, None,
                                  ALU.logical_shift_right).then_inc(ln_step[n], 1)
                k += 1
                dve.wait_ge(ln_step[n], at + k)
                dve.tensor_scalar(b["y"][:, :].bitcast(i32), b["h"][:, :].bitcast(i32), -1.0, RSQRT_SEED,
                                  ALU.mult, ALU.add).then_inc(ln_step[n], 1)
                k += 1
                for _ in range(NEWTON):
                    dve.wait_ge(ln_step[n], at + k)
                    dve.tensor_tensor(b["a"][:, :], b["y"][:, :], b["y"][:, :], ALU.mult).then_inc(ln_step[n], 1)
                    dve.wait_ge(ln_step[n], at + k + 1)
                    dve.tensor_tensor(b["b"][:, :], b["a"][:, :], b["v"][:, :], ALU.mult).then_inc(ln_step[n], 1)
                    dve.wait_ge(ln_step[n], at + k + 2)
                    dve.tensor_scalar(b["c"][:, :], b["b"][:, :], -0.5, 1.5, ALU.mult, ALU.add).then_inc(ln_step[n], 1)
                    dve.wait_ge(ln_step[n], at + k + 3)
                    dve.tensor_tensor(b["y"][:, :], b["y"][:, :], b["c"][:, :], ALU.mult).then_inc(ln_step[n], 1)
                    k += 4
                dve.wait_ge(ln_step[n], at + k)
                assert k == steps
                wait(dve, hi_ready[n], a)
                for t in range(tiles):
                    ins = dve.tensor_scalar(hat[:, t, :], src(t), b["mean"][:, t:t + 1], b["y"][:, t:t + 1],
                                            ALU.subtract, ALU.mult)
                ins.then_inc(hat_ready[n], 1)

            def lo_part(n, a, src, dst):
                dve.wait_ge(hi_ready[n], a + 1)
                dve.tensor_tensor(dst[:, 1], src[:, :, :], dst[:, 0], ALU.subtract).then_inc(lo_ready[n], 1)

            def gain(n, g, group):
                dve.wait_ge(bias_mm[group], 1)
                for c in range(KT):
                    dve.tensor_scalar(wraw[n][:, c, :], wraw[n][:, c, :], lng[g][:, c:c + 1], None, ALU.mult)\
                        .then_inc(gained[group], 1)

            def magnitude(col, group, src, axis):
                dve.tensor_reduce(amax[group][:, col:col + 1], src, axis, ALU.max, apply_absolute_value=True)\
                    .then_inc(amax_ready[group], 1)

            def scales(group, lo, hi, pairs):
                s, m = scale_step[group], amax_all[group]
                dve.wait_ge(amax_shared[group], 1)
                if group == "a":
                    dve.tensor_tensor(mag[:, 0:3], m[:, 0:3], m[:, 3:6], ALU.max).then_inc(s, 1)
                    k = 1
                else:
                    dve.tensor_tensor(mag[:, 3:4], m[:, 0:1], m[:, 3:4], ALU.max).then_inc(s, 1)
                    dve.tensor_copy(mag[:, 4:6], m[:, 1:3]).then_inc(s, 1)
                    k = 2
                dve.wait_ge(s, k)
                dve.tensor_scalar(pow2[:, lo:hi], mag[:, lo:hi], 1e-30, None, ALU.max).then_inc(s, 1)
                dve.wait_ge(s, k + 1)
                dve.tensor_scalar(inv[:, lo:hi].bitcast(i32), pow2[:, lo:hi].bitcast(i32), 0x7F800000, None,
                                  ALU.bitwise_and).then_inc(s, 1)
                dve.wait_ge(s, k + 2)
                dve.tensor_scalar(scale_dn[:, lo:hi], inv[:, lo:hi], 1.0 / 16, None, ALU.mult).then_inc(s, 1)
                dve.wait_ge(s, k + 3)
                dve.reciprocal(scale_up[:, lo:hi], scale_dn[:, lo:hi]).then_inc(s, 1)
                dve.wait_ge(s, k + 4)

            def weight_lo(n, src):
                dve.wait_ge(whi_ready[n], 1)
                dve.scalar_tensor_tensor(wp[n][:, 1].rearrange("p c n -> p (c n)"),
                                         src.rearrange("p c n -> p (c n)"), scale_up[:, COL[n]:COL[n] + 1],
                                         wp[n][:, 0].rearrange("p c n -> p (c n)"),
                                         ALU.mult, ALU.subtract).then_inc(wlo_ready[n], 1)

            dve.wait_ge(ld_cols, 16)
            dve.tensor_copy(lnb1_rep[:, :, :], lnb[1][:, :, None].broadcast_to([P, KT, P])).then_inc(lnb_rep_ready, 1)
            dve.wait_ge(ld_c[0], 16)
            dve.wait_ge(ld_c[1], 16)
            layer_norm("c", 0, lambda t: c_sb[:, t, :], CTT, c_hat)
            for n in ("k", "v", "q"):
                gain(n, 1, "a")
            dve.wait_ge(gained["a"], 3 * KT)
            for n in ("q", "k", "v"):
                magnitude(COL[n], "a", wraw[n][:, :, :], AX.XY)
            dve.wait_ge(ld_cols, 16)
            dve.tensor_tensor(bfull["q"][:, :], bank[:, 0, 0:KT], bcol["q"][:, :], ALU.add).then_inc(consts_ready, 1)
            dve.tensor_tensor(bfull["k"][:, :], bank[:, 0, KT:2 * KT], bcol["k"][:, :], ALU.add)\
                .then_inc(consts_ready, 1)
            dve.wait_ge(ld_rows, 16)
            dve.tensor_tensor(bv_full[:, :], bank[:, 1, 0:E], brow["v"][:, :], ALU.add).then_inc(consts_ready, 1)
            dve.wait_ge(consts_ready, 4)
            magnitude(3, "a", bfull["q"][:, :], AX.X)
            magnitude(4, "a", bfull["k"][:, :], AX.X)
            magnitude(5, "a", bv_full[:, :], AX.X)
            lo_part("c", 0, c_hat, c_parts)
            dve.wait_ge(pool_const, 12)
            for u in range(2):
                dve.tensor_reduce(evenodd[:, u:u + 1], blocks[:, u:8:2], AX.X, ALU.add).then_inc(consts_ready, 1)
            scales("a", 0, 3, None)
            for n in ("q", "k"):
                dve.tensor_scalar(bscaled[n][:, :], bfull[n][:, :], scale_up[:, COL[n]:COL[n] + 1], None, ALU.mult)
            dve.tensor_scalar(bv_scaled[:, :], bv_full[:, :], scale_up[:, 2:3], None, ALU.mult)
            dve.tensor_tensor(sc_exp0[:, :], scale_dn[:, 0:1], scale_dn[:, 1:2], ALU.mult)\
                .then_inc(scales_ready["a"], 1)
            dve.wait_ge(scales_ready["a"], 1)
            dve.tensor_scalar(sc_exp[:, :], sc_exp0[:, :], float(HD) ** -0.5, None, ALU.mult)\
                .then_inc(scales_ready["a"], 1)
            for n in ("k", "v", "q"):
                weight_lo(n, wraw[n][:, :, :])
            for t in range(CTT):
                dve.wait_ge(cT_hi, t + 1)
                dve.tensor_copy(cT[:, 1, :, t * P:CSTART[t] + P],
                                half16(t % 4)[:, 2 * P:4 * P].rearrange("p (k n) -> p k n", k=KT)
                                [:, :, t * P - CSTART[t]:]).then_inc(cT_lo, 1)
            for h in range(KT):
                for c in range(2):
                    dve.wait_ge(khi_ready, 2 * h + c + 1)
                    dve.scalar_tensor_tensor(k_lo[:, h, c * CCH:(c + 1) * CCH], bank[:, 4 + 2 * h + c, 0:CCH],
                                             bscaled["k"][:, h:h + 1], k_hi[:, h, c * CCH:(c + 1) * CCH],
                                             ALU.add, ALU.subtract).then_inc(klo_ready, 1)
            dve.wait_ge(ld_x[0], 16)
            layer_norm("1", 0, lambda t: x_sb[:, t, :], TT, x_hat)
            for b in range(NBATCH // 2):
                dve.wait_ge(v_mm, b + 1)
                dve.tensor_tensor(v_all[:, 2 * b:2 * b + 2, :], bank[0:SK, b, :].rearrange("p (b n) -> p b n", b=2),
                                  bv_scaled[0:SK, None, :].broadcast_to([SK, 2, E]), ALU.add).then_inc(v_ready, 1)
            lo_part("1", 0, x_hat, x_parts)

            def front(a):
                dve.wait_ge(xT_done, 2 * a + 2)
                dve.tensor_copy(xT[:, 1, :, :], half16(1).rearrange("p (k n) -> p k n", k=KT)).then_inc(xT_lo, 1)
                for h in range(KT):
                    dve.wait_ge(qhi_ready, a * KT + h + 1)
                    dve.scalar_tensor_tensor(q_lo[:, h, :], bank[:, 2 + h, :], bscaled["q"][:, h:h + 1],
                                             q_hi[:, h, :], ALU.add, ALU.subtract).then_inc(qlo_ready, 1)

            def maxima(a, t):
                for n, groups in enumerate(FILLS):
                    fill = len(FILLS) * t + n
                    dve.wait_ge(s_done, a * NF + fill + 1)
                    s0, s1 = 2 * groups[0], 2 * groups[-1] + 2
                    dve.tensor_reduce(smax[:, t, s0:s1],
                                      bank[:, fill % 4, 0:(s1 - s0) * SK].rearrange("p (h k) -> p h k", k=SK),
                                      AX.X, ALU.max).then_inc(smax_ready, 1)

            def max_rows(a):
                dve.wait_ge(smax_ready, (a + 1) * NF)
                dve.tensor_scalar(m_parts[:, :, 0, :], smax[:, :, :], -1.0 / SEL, None, ALU.mult)\
                    .then_inc(mhi_ready, 1)
                dve.wait_ge(mhi_ready, a + 1)
                dve.scalar_tensor_tensor(m_parts[:, :, 1, :], smax[:, :, :], -1.0 / SEL, m_parts[:, :, 0, :],
                                         ALU.mult, ALU.subtract).then_inc(m_ready, 1)
                dve.wait_ge(mT_done, a + 1)
                dve.tensor_copy(mT[96:128, :], half16(4)[0:32, 0:TOK]).then_inc(mT_copied, 1)
                dve.wait_ge(mT_copied, a + 1)
                dve.tensor_copy(qpack[96:128, :, :], mT[96:128, None, :].broadcast_to([32, NG, TOK]))\
                    .then_inc(m_rows, 1)

            def back(a):
                for t in range(TT):
                    dve.wait_ge(on_done, TT * a + t + 1)
                    o_ps = bank[:, t, :].rearrange("p (s d) -> p s d", d=32)
                    dve.reciprocal(rden[:, t, :], o_ps[:, :, HD]).then_inc(rden_ready, 1)
                    dve.wait_ge(rden_ready, TT * a + t + 1)
                    dve.tensor_tensor(o_nat[:, t, :].rearrange("p (s d) -> p s d", d=HD), o_ps[:, :, 0:HD],
                                      rden[:, t, :, None].broadcast_to([P, H, HD]), ALU.mult).then_inc(onat_ready, 1)
                lo_part("o", a, o_nat, o_parts)
                dve.wait_ge(onT_done, 2 * a + 2)
                dve.tensor_copy(onT[:, 1, :, :], half16(5).rearrange("p (k n) -> p k n", k=KT)).then_inc(onT_lo, 1)
                dve.wait_ge(xres_ready, a + 1)
                wait(dve, x1res_ready, a)
                for t in range(TT):
                    dve.wait_ge(wo_done, TT * a + t + 1)
                    dve.scalar_tensor_tensor(x1[:, t, :], bank[:, t, 0:E], sc_vo[:, :], x_res[:, t, :],
                                             ALU.mult, ALU.add).then_inc(x1_ready, 1)
                dve.wait_ge(x1_ready, TT * a + TT)
                layer_norm("2", a, lambda t: x1[:, t, :], TT, y_hat)
                lo_part("2", a, y_hat, y_parts)

            def mlp_front(f):
                dve.wait_ge(yT_done, 2 * f + 2)
                dve.tensor_copy(yT[:, 1, :, :], half16(5).rearrange("p (k n) -> p k n", k=KT)).then_inc(yT_lo, 1)

            def gelu_lo(f, m):
                dve.wait_ge(ghi_ready, f * MT + m + 1)
                dve.scalar_tensor_tensor(g_lo[:, m, :], g_full[:, m % 2, :], scale_up[:, 3:4], g_hi[:, m, :],
                                         ALU.mult, ALU.subtract).then_inc(glo_ready, 1)

            def outputs(f, t):
                if t == 0:
                    dve.wait_ge(x1res_ready, f + 1)
                dve.wait_ge(f2_done, f * TT + t + 1)
                dve.scalar_tensor_tensor(x1_res[:, t, :], bank[:, 6 + t % 2, 0:E], sc_12[:, :], x1_res[:, t, :],
                                         ALU.mult, ALU.add).then_inc(out_ready, 1)

            def norm_x(a):
                layer_norm("1", a, lambda t: x_sb[:, bass.ds(a * TT + t, 1), :], TT, x_hat)
                lo_part("1", a, x_hat, x_parts)

            front(0)
            dve.wait_ge(kpack_loaded, 24 * 16)
            dve.wait_ge(consts_ready, 6)
            for u in range(2):
                dve.tensor_scalar(kpack[:, u:H:2, :], kpack[:, u:H:2, :], evenodd[0:96, u:u + 1], None, ALU.mult)\
                    .then_inc(kpack_masked, 1)
            dve.wait_ge(ld_cols, 16)
            gain("1", 2, "b")
            dve.wait_ge(gained["b"], KT)
            magnitude(0, "b", wraw["1"][:, :, :], AX.XY)
            dve.wait_ge(ld_w["o"], 64)
            magnitude(1, "b", wraw["o"][:, :, :], AX.XY)
            dve.wait_ge(ld_w["2"], 16)
            magnitude(2, "b", wraw["2"][:, :, :], AX.XY)
            dve.wait_ge(ld_cols, 16)
            dve.tensor_tensor(bfull["1"][:, :], bank[:, 6, 0:MT], bcol["1"][:, :], ALU.add).then_inc(consts_ready, 1)
            dve.wait_ge(consts_ready, 7)
            magnitude(3, "b", bfull["1"][:, :], AX.X)
            for t in range(TT):
                maxima(0, t)
            max_rows(0)
            scales("b", 3, 6, None)
            dve.tensor_tensor(sc_vo[:, :], scale_dn[:, 2:3], scale_dn[:, 4:5], ALU.mult)
            dve.tensor_tensor(sc_12[:, :], scale_dn[:, 3:4], scale_dn[:, 5:6], ALU.mult)\
                .then_inc(scales_ready["b"], 1)
            for n, src in (("o", wraw["o"]), ("1", wraw["1"]), ("2", wraw["2"])):
                weight_lo(n, src[:, :, :])
            for i in range(1, PAIRS):
                dve.wait_ge(ld_x[i], 16)
            norm_x(1)
            dve.wait_ge(scales_ready["b"], 1)
            back(0)

            def both(i, last=False):
                front(i + 1)
                mlp_front(i)
                for m in range(MT - 2):
                    gelu_lo(i, m)
                maxima(i + 1, 0)
                gelu_lo(i, MT - 2)
                maxima(i + 1, 1)
                gelu_lo(i, MT - 1)
                maxima(i + 1, 2)
                maxima(i + 1, 3)
                max_rows(i + 1)
                outputs(i, 0)
                outputs(i, 1)
                if not last:
                    norm_x(i + 2)
                outputs(i, 2)
                outputs(i, 3)
                back(i + 1)

            with dve.Fori(0, PAIRS - 2) as i:
                both(i)
            both(PAIRS - 2, last=True)
            mlp_front(PAIRS - 1)
            for m in range(MT):
                gelu_lo(PAIRS - 1, m)
            for t in range(TT):
                outputs(PAIRS - 1, t)

        @block.tensor
        def _(pe):
            def split_product(dst, lhs, rhs, tiles):
                terms = [(c, a, b) for c in range(tiles) for a, b in ((0, 0), (0, 1), (1, 0))]
                for n, (c, a, b) in enumerate(terms):
                    mm = pe.matmul(dst, lhs(a, c), rhs(b, c), start=(n == 0), stop=(n == len(terms) - 1))
                return mm

            def transpose_parts(parts, part, b):
                dst = half16(b).rearrange("p (k n) -> p k n", k=KT)
                for t in range(TT):
                    for c in range(KT):
                        tr = pe.transpose(dst[:, c, t * P:(t + 1) * P], parts[:, part, t, c * P:(c + 1) * P],
                                          ident16[:, :])
                return tr

            pe.wait_ge(lnb_rep_ready, 1)
            for n in ("k", "v", "q"):
                pe.wait_ge(ld_w[n], 16)
            for j, n in enumerate(("q", "k")):
                for h in range(KT):
                    for c in range(KT):
                        pe.matmul(bank[:, 0, j * KT + h:j * KT + h + 1], wraw[n][:, c, h * P:(h + 1) * P],
                                  lnb[1][:, c:c + 1], start=(c == 0), stop=(c == KT - 1))
            for c in range(KT):
                mm = pe.matmul(bank[:, 1, 0:E], lnb1_rep[:, c, :], wraw["v"][:, c, :],
                               start=(c == 0), stop=(c == KT - 1))
            mm.then_inc(bias_mm["a"], 1)

            pe.wait_ge(pool_const, 4)
            pe.wait_ge(hi_ready["c"], 1)
            pe.wait_ge(lo_ready["c"], 1)
            pe.wait_ge(consts_ready, 4)
            for t in range(CTT):
                if t >= 4:
                    pe.wait_ge(cT_lo, t - 3)
                for part in range(2):
                    for c in range(KT):
                        at = (part * KT + c) * P
                        tr = pe.transpose(half16(t % 4)[:, at:at + P], c_parts[:, part, t, c * P:(c + 1) * P],
                                          ident16[:, :])
                tr.then_inc(cT_done, 1)
            pe.wait_ge(cT_lo, CTT)

            pe.wait_ge(wlo_ready["k"], 1)
            for h in range(KT):
                for c in range(2):
                    split_product(bank[:, 4 + 2 * h + c, 0:CCH],
                                  lambda part, k: wp["k"][:, part, k, h * P:(h + 1) * P],
                                  lambda part, k: cT[:, part, k, c * CCH:(c + 1) * CCH], KT).then_inc(k_mm, 1)
            pe.wait_ge(wlo_ready["v"], 1)
            for b in range(NBATCH):
                mm = split_product(bank[0:SK, b // 2, (b % 2) * E:(b % 2 + 1) * E],
                                   lambda part, k: cT[:, part, k, b * SK:(b + 1) * SK],
                                   lambda part, k: wp["v"][:, part, k, :], KT)
                if b % 2:
                    mm.then_inc(v_mm, 1)

            def front(a):
                pe.wait_ge(hi_ready["1"], a + 1)
                wait(pe, onT_lo, a)
                wait(pe, x1_ready, TT * a)
                transpose_parts(x_parts, 0, 0).then_inc(xT_done, 1)
                pe.wait_ge(lo_ready["1"], a + 1)
                transpose_parts(x_parts, 1, 1).then_inc(xT_done, 1)
                pe.wait_ge(xT_hi, a + 1)
                pe.wait_ge(xT_lo, a + 1)
                for h in range(KT):
                    split_product(bank[:, 2 + h, :], lambda part, k: wp["q"][:, part, k, h * P:(h + 1) * P],
                                  lambda part, k: xT[:, part, k, :], KT).then_inc(q_done, 1)

            def scores(a, t):
                kb = t // (TT // 2) * SK
                for n, groups in enumerate(FILLS):
                    fill = len(FILLS) * t + n
                    if fill >= 4:
                        pe.wait_ge(smax_ready, a * NF + fill - 3)
                    elif fill >= 2:
                        pe.wait_ge(qlo_ready, a * KT + fill - 1)
                    for u, g in enumerate(groups):
                        mm = pe.matmul(bank[:, fill % 4, u * SK2:(u + 1) * SK2], qpack[0:96, g, t * P:(t + 1) * P],
                                       k_cur[0:96, 2 * g:2 * g + 2, kb:kb + SK], start=True, stop=True)
                    mm.then_inc(s_done, 1)

            def max_transposed(a):
                pe.wait_ge(m_ready, a + 1)
                for t in range(TT):
                    tr = pe.transpose(half16(4)[0:32, t * P:(t + 1) * P],
                                      m_parts[:, t, :, :].rearrange("p a h -> p (a h)"), ident16[:, :])
                tr.then_inc(mT_done, 1)

            def scores_t(a, s):
                if s == 0:
                    pe.wait_ge(m_rows, a + 1)
                if s < 2:
                    pe.wait_ge(smax_ready, (a + 1) * NF)
                else:
                    pe.wait_ge(exp_done, a * NG + s - 1)
                for u in range(2):
                    for b in range(2):
                        mm = pe.matmul(bank[0:SK, 2 * (s % 2) + u, b * SQ:(b + 1) * SQ],
                                       k_cur[:, 2 * s + u, b * SK:(b + 1) * SK], qpack[:, s, b * SQ:(b + 1) * SQ],
                                       start=True, stop=True)
                mm.then_inc(st_done, 1)

            def values(a, g):
                if g == 0:
                    pe.wait_ge(vcur_ready, a + 1)
                    pe.wait_ge(m_rows, a + 1)
                    wait(pe, yT_lo, a)
                if g >= 2:
                    pe.wait_ge(oT_ready, 4 * a + g - 1)
                pe.wait_ge(exp_done, a * NG + 2 * g + 2)
                for b in range(2):
                    for c in range(4):
                        mm = pe.matmul(bank[32 * c:32 * c + 32, 4 + g % 2, b * SQ:(b + 1) * SQ],
                                       v_cur[:, b, head_of(4 * g + c), :], probs[:, 4 * g + c, b * SQ:(b + 1) * SQ],
                                       start=True, stop=True, tile_position=(0, 32 * c), skip_group_check=True)
                mm.then_inc(pv_done, 1)

            def back(a):
                pe.wait_ge(exp_done, (a + 1) * NG)
                pe.wait_ge(oT_ready, 4 * a + 4)
                for t in range(TT):
                    for g in range(4):
                        tr = pe.transpose(bank[:, t, g * P:(g + 1) * P], oT[:, g, t * P:(t + 1) * P], ident32[:, :])
                    tr.then_inc(on_done, 1)
                pe.wait_ge(hi_ready["o"], a + 1)
                transpose_parts(o_parts, 0, 4).then_inc(onT_done, 1)
                pe.wait_ge(lo_ready["o"], a + 1)
                transpose_parts(o_parts, 1, 5).then_inc(onT_done, 1)
                pe.wait_ge(onT_hi, a + 1)
                pe.wait_ge(onT_lo, a + 1)
                pe.wait_ge(wlo_ready["o"], 1)
                for t in range(TT):
                    split_product(bank[:, t, 0:E], lambda part, k: onT[:, part, k, t * P:(t + 1) * P],
                                  lambda part, k: wp["o"][:, part, k, :], KT).then_inc(wo_done, 1)

            def mlp_front(f):
                pe.wait_ge(hi_ready["2"], f + 1)
                transpose_parts(y_parts, 0, 4).then_inc(yT_done, 1)
                pe.wait_ge(lo_ready["2"], f + 1)
                transpose_parts(y_parts, 1, 5).then_inc(yT_done, 1)
                pe.wait_ge(yT_hi, f + 1)
                pe.wait_ge(yT_lo, f + 1)

            def hidden(f, m):
                if m >= 2:
                    pe.wait_ge(gelu_done, f * MT + m - 1)
                split_product(bank[:, 6 + m % 2, :], lambda part, k: wp["1"][:, part, k, m * P:(m + 1) * P],
                              lambda part, k: yT[:, part, k, :], KT).then_inc(f1_done, 1)

            def mlp_out(f, t):
                if t == 0:
                    pe.wait_ge(gelu_done, f * MT + MT)
                    pe.wait_ge(glo_ready, f * MT + MT)
                if t >= 2:
                    pe.wait_ge(out_ready, f * TT + t - 1)
                split_product(bank[:, 6 + t % 2, 0:E],
                              lambda part, k: (g_hi, g_lo)[part][:, k, t * P:(t + 1) * P],
                              lambda part, k: wp["2"][:, part, k, :], MT).then_inc(f2_done, 1)

            pe.wait_ge(v_ready, NBATCH // 2)
            pe.wait_ge(wlo_ready["q"], 1)
            pe.wait_ge(klo_ready, 2 * KT)
            front(0)
            pe.wait_ge(ld_w["1"], 16)
            pe.wait_ge(ld_cols, 16)
            for m in range(MT):
                for c in range(KT):
                    mm = pe.matmul(bank[:, 6, m:m + 1], wraw["1"][:, c, m * P:(m + 1) * P], lnb[2][:, c:c + 1],
                                   start=(c == 0), stop=(c == KT - 1))
            mm.then_inc(bias_mm["b"], 1)
            pe.wait_ge(kcur_ready, 1)
            pe.wait_ge(qpack_ready, 12 * 16)
            for t in range(TT):
                scores(0, t)
            max_transposed(0)
            for s in range(NG):
                scores_t(0, s)
                if s % 2 and s >= 3:
                    values(0, s // 2 - 1)
            values(0, 3)
            back(0)
            pe.wait_ge(wlo_ready["1"], 1)
            pe.wait_ge(wlo_ready["2"], 1)

            def both(i):
                a = i + 1
                front(a)
                mlp_front(i)
                for m in range(MT - 2):
                    hidden(i, m)
                pe.wait_ge(kcur_ready, a + 1)
                pe.wait_ge(qpack_ready, (a + 1) * 12 * 16)
                scores(a, 0)
                hidden(i, MT - 2)
                scores(a, 1)
                hidden(i, MT - 1)
                scores(a, 2)
                scores(a, 3)
                mlp_out(i, 0)
                mlp_out(i, 1)
                max_transposed(a)
                scores_t(a, 0)
                scores_t(a, 1)
                mlp_out(i, 2)
                scores_t(a, 2)
                scores_t(a, 3)
                values(a, 0)
                mlp_out(i, 3)
                scores_t(a, 4)
                scores_t(a, 5)
                values(a, 1)
                scores_t(a, 6)
                scores_t(a, 7)
                values(a, 2)
                values(a, 3)
                back(a)
                pe.wait_ge(out_ready, i * TT + TT)

            with pe.Fori(0, PAIRS - 1) as i:
                both(i)
            mlp_front(PAIRS - 1)
            for m in range(MT):
                hidden(PAIRS - 1, m)
            for t in range(TT):
                mlp_out(PAIRS - 1, t)


_ORDER = ["x", "ctx_1024"] + ["L0_xattn_" + n for n in ("wq", "wk", "wv", "wo", "w1", "w2")]
_COLUMNS = ["L0_xattn_" + n for n in ("ln1_g", "ln1_b", "ln2_g", "ln2_b", "bq", "bk", "b1")]
_ROWS = ["L0_xattn_" + n for n in ("bv", "bo", "b2")]


def kernel(**inputs):
    import numpy as np
    import concourse.bacc as bacc
    from concourse.bass_utils import run_bass_kernel_spmd

    nc = bacc.Bacc("TRN2", target_bir_lowering=False, num_devices=1)
    arrays, args = {}, []
    laid = {name: np.ascontiguousarray(inputs[name]) for name in _ORDER}
    laid["columns"] = np.ascontiguousarray(np.concatenate([np.asarray(inputs[n]) for n in _COLUMNS]).reshape(-1, 128).T)
    laid["rows"] = np.stack([np.asarray(inputs[n]) for n in _ROWS])
    for name, a in laid.items():
        arrays[f"in_{name}"] = a
        args.append(nc.dram_tensor(f"in_{name}", a.shape, mybir.dt.from_np(a.dtype), kind="ExternalInput").ap())
    out = nc.dram_tensor("out", arrays["in_x"].shape, mybir.dt.float32, kind="ExternalOutput").ap()
    xattn_block_kernel(nc, *args, out)
    r = run_bass_kernel_spmd(nc, [arrays], core_ids=[0])
    return r.results[0]["out"]
```

```python
import concourse.bass as bass
from concourse import mybir
from contextlib import ExitStack



def xattn_block_kernel(nc, x, ctx_in, wq, wk, wv, wo, w1, w2, columns, rows, out):
    f32, f16, i32 = mybir.dt.float32, mybir.dt.float16, mybir.dt.int32
    ALU, ACT, AX = mybir.AluOpType, mybir.ActivationFunctionType, mybir.AxisListType

    NBATCH, SQ, E = x.shape
    SK = ctx_in.shape[1]
    F = w1.shape[1]
    H = 16
    HD = E // H
    P = 128
    KT = E // P
    MT = F // P
    PAIRS = NBATCH // 2
    TOK = 2 * SQ
    TT = TOK // P
    NTOK = NBATCH * SQ
    CTOK = NBATCH * SK
    CSTART = [0, 128, 256, 384, CTOK - P]
    CTT = len(CSTART)
    CCH = CTOK // 2
    SK2 = 2 * SK
    NG = H // 2
    FILLS = [(0, 1, 2), (3, 4, 5), (6, 7)]
    NF = len(FILLS) * TT
    EPS = 1e-5
    SEL = 32768.0
    RSQRT_SEED = float(0x5F3759DF)
    NEWTON = 3
    CONSTS = 13

    def head_of(slot):
        pos = slot // 2
        return 2 * ((pos % 2) * 4 + pos // 2) + slot % 2

    x_t = x.rearrange("b s e -> (b s) e").rearrange("(t p) e -> p t e", p=P)
    out_t = out.rearrange("b s e -> (b s) e").rearrange("(t p) e -> p t e", p=P)
    ctx_rows = ctx_in.rearrange("b s e -> (b s) e")

    stack = ExitStack()
    with stack:
        def sb(name, shape, dt):
            return stack.enter_context(nc.sbuf_tensor(name, shape, dt))

        def sem(name):
            return stack.enter_context(nc.semaphore(name))

        x_sb = sb("x_sb", [P, NTOK // P, E], f32)
        shared = sb("shared", [P, H * TOK], f32)
        shared_g = sb("shared_g", [P, MT * TOK], f32)
        taken = [0]

        def in_shared(dt, words, pattern, **dims):
            view = shared[:, taken[0]:taken[0] + words]
            taken[0] += words
            return (view.bitcast(dt) if dt != f32 else view).rearrange(pattern, **dims)

        c_sb = in_shared(f32, CTT * E, "p (t e) -> p t e", e=E)
        wraw = {n: in_shared(f32, KT * E, "p (c n) -> p c n", n=E) for n in ("q", "k", "v")}
        wraw["o"] = sb("raw_o", [P, KT, E], f32)
        wraw["1"] = shared_g[:, 0:KT * F].rearrange("p (c n) -> p c n", n=F)
        wraw["2"] = shared_g[:, KT * F:KT * F + MT * E].rearrange("p (c n) -> p c n", n=E)
        wp = {n: sb(f"parts_{n}", [P, 2] + list(wraw[n].shape[1:]), f16) for n in wraw}
        cols = sb("cols", [P, 6 * KT + MT], f32)
        lng = {1: cols[:, 0:KT], 2: cols[:, 2 * KT:3 * KT]}
        lnb = {1: cols[:, KT:2 * KT], 2: cols[:, 3 * KT:4 * KT]}
        bcol = {"q": cols[:, 4 * KT:5 * KT], "k": cols[:, 5 * KT:6 * KT], "1": cols[:, 6 * KT:6 * KT + MT]}
        brows = sb("brows", [P, 3, E], f32)
        brow = {n: brows[:, j, :] for j, n in enumerate(("v", "o", "2"))}
        lnb1_rep = in_shared(f32, KT * P, "p (c n) -> p c n", n=P)
        bfull = {n: sb(f"bfull_{n}", [P, MT if n == "1" else KT], f32) for n in bcol}
        bscaled = {n: sb(f"bscaled_{n}", [P, KT], f32) for n in ("q", "k")}
        bv_full = sb("bv_full", [P, E], f32)
        bv_scaled = sb("bv_scaled", [P, E], f32)
        amax = {"a": sb("amax_a", [P, 6], f32), "b": sb("amax_b", [P, 4], f32)}
        amax_all = {"a": sb("amax_all_a", [P, 6], f32), "b": sb("amax_all_b", [P, 4], f32)}
        mag = sb("mag", [P, 6], f32)
        pow2 = sb("pow2", [P, 6], f32)
        inv = sb("inv", [P, 6], f32)
        scale_up = sb("scale_up", [P, 6], f32)
        scale_dn = sb("scale_dn", [P, 6], f32)
        sc_exp0 = sb("sc_exp0", [P, 1], f32)
        sc_exp = sb("sc_exp", [P, 1], f32)
        sc_vo = sb("sc_vo", [P, 1], f32)
        sc_12 = sb("sc_12", [P, 1], f32)
        COL = {"q": 0, "k": 1, "v": 2, "1": 3, "o": 4, "2": 5}

        ident16 = sb("ident16", [P, P], f16)
        ident32 = sb("ident32", [P, P], f32)
        blocks = sb("blocks", [P, 8], f32)
        evenodd = sb("evenodd", [P, 2], f32)
        selector = sb("selector", [P, H], f16)
        zero = sb("zero", [P, 1], f32)

        c_hat = in_shared(f32, CTT * E, "p (t e) -> p t e", e=E)
        c_parts = in_shared(f16, CTT * E, "p (a t e) -> p a t e", a=2, e=E)
        cT = in_shared(f16, KT * CTOK, "p (a k n) -> p a k n", a=2, k=KT)
        k_hi = in_shared(f16, KT * CTOK // 2, "p (k n) -> p k n", k=KT)
        k_lo = in_shared(f16, KT * CTOK // 2, "p (k n) -> p k n", k=KT)
        pack = sb("pack", [P, H, CTOK], f16)
        kpack = pack[0:96, :, :]
        v_all = sb("v_all", [SK, NBATCH, E], f32)
        k_cur = sb("k_cur", [P, H, SK2], f16)
        v_cur = sb("v_cur", [SK, 2, H, 32], f32)
        x_hat = sb("x_hat", [P, TT, E], f32)
        x_parts = sb("x_parts", [P, 2, TT, E], f16)
        xT = sb("xT", [P, 2, KT, TOK], f16)
        q_hi = sb("q_hi", [P, KT, TOK], f16)
        q_lo = sb("q_lo", [P, KT, TOK], f16)
        qpack = sb("qpack", [P, NG, TOK], f16)
        smax = sb("smax", [P, TT, H], f32)
        m_parts = sb("m_parts", [P, TT, 2, H], f16)
        mT = pack[:, 0, 0:TOK]
        probs = shared[0:SK, :].rearrange("p (h n) -> p h n", h=H)
        oT = sb("oT", [P, 4, TOK], f32)
        rden = sb("rden", [P, TT, H], f32)
        o_nat = sb("o_nat", [P, TT, E], f32)
        o_parts = sb("o_parts", [P, 2, TT, E], f16)
        onT = sb("onT", [P, 2, KT, TOK], f16)
        x_res = sb("x_res", [P, TT, E], f32)
        x1 = sb("x1", [P, TT, E], f32)
        x1_res = sb("x1_res", [P, TT, E], f32)
        y_hat = sb("y_hat", [P, TT, E], f32)
        y_parts = sb("y_parts", [P, 2, TT, E], f16)
        yT = sb("yT", [P, 2, KT, TOK], f16)
        g_full = sb("g_full", [P, 2, TOK], f32)
        g_parts = shared_g[:, :].bitcast(f16).rearrange("p (a m n) -> p a m n", a=2, m=MT)
        g_hi, g_lo = g_parts[:, 0], g_parts[:, 1]
        def ln_buffers(n, w):
            small = {x: sb(f"ln{n}_{x}", [P, w], f32) for x in ("mean", "v", "h", "a", "b", "c", "y")}
            return dict(st=sb(f"ln{n}_st", [P, w, 6], f32), **small)

        ln_buf = {"rest": ln_buffers("rest", (PAIRS - 1) * TT), "2": ln_buffers("2", TT)}
        for n, w in (("c", CTT), ("1", TT)):
            ln_buf[n] = {x: t[:, 0:w] if x != "st" else t[:, 0:w, :] for x, t in ln_buf["rest"].items()}

        bank = stack.enter_context(nc.psum_tensor("bank", [P, 8, 512], f32))

        def half16(b):
            return bank[:, b, :].bitcast(f16)

        def transposed(half):
            return half16(4 + half).rearrange("p (a k n) -> p a k n", a=2, k=KT)

        ld_c = [sem(f"ld_c{i}") for i in range(2)]
        ld_x = [sem(f"ld_x{i}") for i in range(PAIRS)]
        ld_w = {n: sem(f"ld_w{n}") for n in wraw}
        ld_cols, ld_rows = sem("ld_cols"), sem("ld_rows")
        pool_const = sem("pool_const")
        consts_ready = sem("consts_ready")
        lnb_rep_ready = sem("lnb_rep_ready")
        ln_step = {n: sem(f"ln_step_{n}") for n in ("c", "1", "rest", "2")}
        hat_ready = {n: sem(f"hat_ready_{n}") for n in ("c", "1", "2")}
        hi_ready = {n: sem(f"hi_ready_{n}") for n in ("c", "1", "2", "o")}
        rest_ready = sem("rest_ready")
        centred = sem("centred")
        lo_ready = {n: sem(f"lo_ready_{n}") for n in ("c", "1", "2", "o")}
        cT_done, cT_hi, cT_lo = sem("cT_done"), sem("cT_hi"), sem("cT_lo")
        bias_mm = {"a": sem("bias_mm_a"), "b": sem("bias_mm_b")}
        gained = {"a": sem("gained_a_ready"), "b": sem("gained_b_ready")}
        amax_ready = {"a": sem("amax_ready_a"), "b": sem("amax_ready_b")}
        amax_shared = {"a": sem("amax_shared_a"), "b": sem("amax_shared_b")}
        scale_step = {"a": sem("scale_step_a"), "b": sem("scale_step_b")}
        scales_ready = {"a": sem("scales_ready_a"), "b": sem("scales_ready_b")}
        whi_ready = {n: sem(f"whi_{n}") for n in wraw}
        wlo_ready = {n: sem(f"wlo_{n}") for n in wraw}
        k_mm, khi_ready, klo_ready = sem("k_mm"), sem("khi_ready"), sem("klo_ready")
        kpack_loaded, kpack_masked = sem("kpack_loaded"), sem("kpack_masked")
        v_mm, v_ready = sem("v_mm"), sem("v_ready")
        kcur_ready, vcur_ready = sem("kcur_ready"), sem("vcur_ready")
        xres_ready, x1res_ready = sem("xres_ready"), sem("x1res_ready")
        xT_done, xT_ready = sem("xT_done"), sem("xT_ready")
        q_done, qhi_ready, qlo_ready = sem("q_done"), sem("qhi_ready"), sem("qlo_ready")
        qpack_ready = sem("qpack_ready")
        s_done, smax_ready = sem("s_done"), sem("smax_ready")
        mhi_ready, m_ready, mT_done, mT_copied, m_rows = [sem(n) for n in (
            "mhi_ready", "m_ready", "mT_done", "mT_copied", "m_rows")]
        st_done, exp_done = sem("st_done"), sem("exp_done")
        pv_done, oT_ready = sem("pv_done"), sem("oT_ready")
        on_done, rden_ready, onat_ready = sem("on_done"), sem("rden_ready"), sem("onat_ready")
        onT_done, onT_first, onT_second = sem("onT_done"), sem("onT_first"), sem("onT_second")
        wo_done, x1_ready = sem("wo_done"), sem("x1_ready")
        yT_done, yT_first, yT_second = sem("yT_done"), sem("yT_first"), sem("yT_second")
        f1_done, gelu_done, ghi_ready, glo_ready = [sem(n) for n in ("f1_done", "gelu_done", "ghi_ready", "glo_ready")]
        f2_done, out_ready, out_stored = sem("f2_done"), sem("out_ready"), sem("out_stored")

        block = stack.enter_context(nc.Block())

        def wait(eng, s, value):
            if isinstance(value, int) and value <= 0:
                return
            eng.wait_ge(s, value)

        @block.sync
        def _(sp):
            for i, (lo, hi) in enumerate(((0, 4), (4, 5))):
                src = ctx_rows[0:4 * P, :].rearrange("(t p) e -> p t e", p=P) if i == 0 else \
                    ctx_rows[CTOK - P:CTOK, :].rearrange("(t p) e -> p t e", p=P)
                sp.dma_start(c_sb[:, lo:hi, :], src).then_inc(ld_c[i], 16)
            for n, w in (("k", wk), ("v", wv), ("q", wq)):
                sp.dma_start(wraw[n][:, :, :], w.rearrange("(c p) n -> p c n", p=P)).then_inc(ld_w[n], 16)
            sp.dma_start(x_sb[:, 0:TT, :], x_t[:, 0:TT, :]).then_inc(ld_x[0], 16)
            for hh in range(2):
                for c1 in range(2):
                    src = wo.rearrange("(c k h r) n -> c h r k n", c=2, k=2, h=2)[c1, hh]
                    at = hh * 64 + c1 * 32
                    sp.dma_start(wraw["o"][at:at + 32, :, :], src).then_inc(ld_w["o"], 16)
            sp.dma_start(wraw["1"][:, :, :], w1.rearrange("(c p) n -> p c n", p=P)).then_inc(ld_w["1"], 16)
            sp.dma_start(wraw["2"][:, :, :], w2.rearrange("(c p) n -> p c n", p=P)).then_inc(ld_w["2"], 16)

            for part, src in ((0, k_hi), (1, k_lo)):
                for j in range(4):
                    sp.wait_ge(khi_ready, 2 * KT) if part == 0 else sp.wait_ge(klo_ready, 2 * KT)
                    for role in ((0, 1) if part == 0 else (2,)):
                        for u in range(2):
                            dst = kpack[32 * role:32 * role + 32, 4 * j + u:4 * j + u + 3:2, :]
                            sp.dma_start(dst, src[32 * j:32 * j + 32, :, :]).then_inc(kpack_loaded, 16)
            for i in range(1, PAIRS):
                sp.dma_start(x_sb[:, i * TT:(i + 1) * TT, :], x_t[:, i * TT:(i + 1) * TT, :]).then_inc(ld_x[i], 16)

            def pack_q(a):
                wait(sp, st_done, a * NG)
                for part, src in ((0, q_hi), (1, q_lo)):
                    sp.wait_ge((qhi_ready, qlo_ready)[part], a * KT + KT)
                    for role in ((0, 2) if part == 0 else (1,)):
                        for j in range(4):
                            sp.dma_start(qpack[32 * role:32 * role + 32, 2 * j:2 * j + 2, :],
                                         src[32 * j:32 * j + 32, :, :]).then_inc(qpack_ready, 16)

            def store(f, t0, t1):
                for t in range(t0, t1):
                    sp.wait_ge(out_ready, f * TT + t + 1)
                    sp.dma_start(out_t[:, bass.ds(f * TT + t, 1), :], x1_res[:, t:t + 1, :]).then_inc(out_stored, 16)

            pack_q(0)
            pack_q(1)
            with sp.Fori(0, PAIRS - 2) as i:
                store(i, 0, 1)
                pack_q(i + 2)
                store(i, 1, TT)
            store(PAIRS - 2, 0, TT)
            store(PAIRS - 1, 0, TT)
            sp.wait_ge(out_stored, 16 * TT * PAIRS)

        @block.gpsimd
        def _(pool):
            made = [0]

            def const_step(ins):
                made[0] += 1
                ins.then_inc(pool_const, 1)
                pool.wait_ge(pool_const, made[0])

            for m in (ident16, ident32):
                const_step(pool.memset(m[:, :], 0.0))
                const_step(pool.affine_select(out=m[:, :], in_=m[:, :], compare_op=ALU.not_equal, fill=1.0, base=0,
                                              pattern=[[-1, P]], channel_multiplier=1))
            const_step(pool.memset(blocks[:, :], 1.0))
            const_step(pool.affine_select(out=blocks[:, :], in_=blocks[:, :], compare_op=ALU.is_ge, fill=0.0,
                                          base=0, pattern=[[-16, 8]], channel_multiplier=1))
            const_step(pool.affine_select(out=blocks[:, :], in_=blocks[:, :], compare_op=ALU.is_ge, fill=0.0,
                                          base=15, pattern=[[16, 8]], channel_multiplier=-1))
            const_step(pool.memset(selector[96:128, :], 0.0))
            for first in (0, 16):
                const_step(pool.affine_select(out=selector[96:128, :], in_=selector[96:128, :],
                                              compare_op=ALU.not_equal, fill=SEL, base=-first,
                                              pattern=[[-1, H]], channel_multiplier=1))
            const_step(pool.memset(zero[:, :], 0.0))
            const_step(pool.memset(v_cur[:, :, :, :], 0.0))
            const_step(pool.memset(v_cur[:, :, :, HD:HD + 1], 1.0))
            for g in ("a", "b"):
                pool.wait_ge(amax_ready[g], 6 if g == "a" else 4)
                pool.partition_all_reduce(amax_all[g][:, :], amax[g][:, :], P,
                                          bass.bass_isa.ReduceOp.max).then_inc(amax_shared[g], 1)
                pool.wait_ge(amax_shared[g], 1)

            def copy_kv(a):
                wait(pool, st_done, a * NG)
                pool.tensor_copy(k_cur[0:96, :, :].bitcast(i32),
                                 kpack[:, :, bass.ds(a * SK2, SK2)].bitcast(i32)).then_inc(kcur_ready, 1)
                pool.wait_ge(kcur_ready, a + 1)
                wait(pool, pv_done, a * 4)
                pool.tensor_copy(v_cur[:, :, :, 0:HD],
                                 v_all[:, bass.ds(2 * a, 2), :].rearrange("p b (h d) -> p b h d", h=H))\
                    .then_inc(vcur_ready, 1)
                pool.wait_ge(ld_rows, 16)
                pool.wait_ge(vcur_ready, a + 1)
                wait(pool, x1_ready, a * TT)
                pool.tensor_tensor(x_res[:, :, :], x_sb[:, bass.ds(a * TT, TT), :],
                                   brow["o"][:, None, :].broadcast_to([P, TT, E]), ALU.add).then_inc(xres_ready, 1)
                pool.wait_ge(xres_ready, a + 1)

            def x1_with_bias(a):
                pool.wait_ge(x1_ready, a * TT + TT)
                wait(pool, out_stored, a * TT * 16)
                pool.tensor_tensor(x1_res[:, :, :], x1[:, :, :],
                                   brow["2"][:, None, :].broadcast_to([P, TT, E]), ALU.add).then_inc(x1res_ready, 1)
                pool.wait_ge(x1res_ready, a + 1)

            def normalise_x(a):
                pool.wait_ge(hi_ready["1"], a)
                pool.wait_ge(lo_ready["1"], a)
                pool.tensor_tensor(x_hat[:, :, :], x_sb[:, bass.ds(a * TT, TT), :],
                                   ln_buf["rest"]["mean"][:, bass.ds((a - 1) * TT, TT), None].broadcast_to([P, TT, E]),
                                   ALU.subtract).then_inc(centred, 1)
                pool.wait_ge(centred, a)
                pool.tensor_tensor(x_hat[:, :, :], x_hat[:, :, :],
                                   ln_buf["rest"]["y"][:, bass.ds((a - 1) * TT, TT), None].broadcast_to([P, TT, E]),
                                   ALU.mult).then_inc(hat_ready["1"], 1)
                pool.wait_ge(hat_ready["1"], a + 1)
                pool.wait_ge(xT_done, 2 * a)
                pool.tensor_tensor(x_parts[:, 0], x_hat[:, :, :], zero[:, :, None].broadcast_to([P, TT, E]), ALU.add)\
                    .then_inc(hi_ready["1"], 1)
                pool.wait_ge(hi_ready["1"], a + 1)
                pool.tensor_tensor(x_parts[:, 1], x_hat[:, :, :], x_parts[:, 0], ALU.subtract)\
                    .then_inc(lo_ready["1"], 1)
                pool.wait_ge(lo_ready["1"], a + 1)

            pool.wait_ge(kpack_masked, 2)
            pool.wait_ge(v_ready, NBATCH // 2)
            pool.wait_ge(ld_rows, 16)
            for i in range(PAIRS):
                pool.wait_ge(ld_x[i], 16)
            copy_kv(0)
            pool.wait_ge(rest_ready, 1)
            normalise_x(1)
            copy_kv(1)
            x1_with_bias(0)
            with pool.Fori(0, PAIRS - 2) as i:
                normalise_x(i + 2)
                copy_kv(i + 2)
                x1_with_bias(i + 1)
            x1_with_bias(PAIRS - 1)

        @block.scalar
        def _(act):
            def hi_part(n, a, src, dst):
                act.wait_ge(hat_ready[n], a + 1)
                act.activation(dst[:, 0], src[:, :, :], ACT.Copy).then_inc(hi_ready[n], 1)

            act.dma_start(cols[:, :], columns).then_inc(ld_cols, 16)
            act.dma_start(brows[:, :, :], rows.partition_broadcast(P)).then_inc(ld_rows, 16)
            act.wait_ge(pool_const, CONSTS)
            act.activation(k_cur[96:128, :, :], selector[96:128, :, None].broadcast_to([32, H, SK2]),
                           ACT.Copy).then_inc(consts_ready, 1)
            hi_part("c", 0, c_hat, c_parts)
            for n in ("k", "v", "q"):
                if n == "k":
                    act.wait_ge(scales_ready["a"], 1)
                    act.wait_ge(gained["a"], 2 * KT + KT)
                act.activation(wp[n][:, 0], wraw[n][:, :, :], ACT.Copy, scale=scale_up[:, COL[n]:COL[n] + 1])\
                    .then_inc(whi_ready[n], 1)
            for t in range(CTT):
                act.wait_ge(cT_done, t + 1)
                act.activation(cT[:, 0, :, t * P:CSTART[t] + P],
                               half16(t % 4)[:, 0:2 * P].rearrange("p (k n) -> p k n", k=KT)
                               [:, :, t * P - CSTART[t]:], ACT.Copy)\
                    .then_inc(cT_hi, 1)
            for h in range(KT):
                for c in range(2):
                    act.wait_ge(k_mm, 2 * h + c + 1)
                    act.activation(k_hi[:, h, c * CCH:(c + 1) * CCH], bank[:, 4 + 2 * h + c, 0:CCH], ACT.Identity,
                                   bias=bscaled["k"][:, h:h + 1]).then_inc(khi_ready, 1)

            def queries_hi(a, h):
                if h == 0:
                    wait(act, qpack_ready, a * 12 * 16)
                act.wait_ge(q_done, a * KT + h + 1)
                act.activation(q_hi[:, h, :], bank[:, 4 + h, :], ACT.Identity, bias=bscaled["q"][:, h:h + 1])\
                    .then_inc(qhi_ready, 1)

            def weights_b(n):
                act.activation(wp[n][:, 0], wraw[n][:, :, :], ACT.Copy, scale=scale_up[:, COL[n]:COL[n] + 1])\
                    .then_inc(whi_ready[n], 1)

            def exps(a, s0, s1):
                for s in range(s0, s1):
                    act.wait_ge(st_done, a * NG + s + 1)
                    b0 = 2 * (s % 2)
                    act.activation(probs[:, 2 * s:2 * s + 2, :], bank[0:SK, b0:b0 + 2, :], ACT.Exp,
                                   scale=sc_exp[0:SK, :]).then_inc(exp_done, 1)

            def copy_o(a, g):
                act.wait_ge(pv_done, 4 * a + g + 1)
                act.activation(oT[:, g, :], bank[:, 4 + g % 2, :], ACT.Copy).then_inc(oT_ready, 1)

            def back(a):
                for t in range(TT):
                    act.wait_ge(onat_ready, TT * a + t + 1)
                    act.activation(o_parts[:, 0, t, :], o_nat[:, t, :], ACT.Copy).then_inc(hi_ready["o"], 1)
                act.wait_ge(onT_done, 2 * a + 1)
                act.activation(onT[:, :, :, 0:SQ], transposed(0), ACT.Copy).then_inc(onT_first, 1)

            def split_y(a):
                for t in range(TT):
                    act.wait_ge(hat_ready["2"], TT * a + t + 1)
                    act.activation(y_parts[:, 0, t, :], y_hat[:, t, :], ACT.Copy).then_inc(hi_ready["2"], 1)

            def mlp_front(f):
                act.wait_ge(yT_done, 2 * f + 1)
                act.activation(yT[:, :, :, 0:SQ], transposed(0), ACT.Copy).then_inc(yT_first, 1)

            def gelus(f, m0, m1):
                for m in range(m0, m1):
                    act.wait_ge(f1_done, f * MT + m + 1)
                    if m >= 2:
                        act.wait_ge(glo_ready, f * MT + m - 1)
                    act.activation(g_full[:, m % 2, :], bank[:, 6 + m % 2, :], ACT.Gelu,
                                   bias=bfull["1"][:, m:m + 1], scale=scale_dn[:, 3:4]).then_inc(gelu_done, 1)
                    act.wait_ge(gelu_done, f * MT + m + 1)
                    act.activation(g_hi[:, m, :], g_full[:, m % 2, :], ACT.Copy, scale=scale_up[:, 3:4])\
                        .then_inc(ghi_ready, 1)

            def pair(a, mlp=True, nxt=True):
                if mlp:
                    mlp_front(a - 1)
                    gelus(a - 1, 0, MT)
                exps(a, 0, 2)
                if nxt:
                    queries_hi(a + 1, 0)
                exps(a, 2, 3)
                if nxt:
                    queries_hi(a + 1, 1)
                exps(a, 3, 6)
                copy_o(a, 0)
                exps(a, 6, 8)
                for g in range(1, 4):
                    copy_o(a, g)
                back(a)
                split_y(a)

            act.wait_ge(hat_ready["1"], 1)
            act.activation(x_parts[:, 0], x_hat[:, :, :], ACT.Copy).then_inc(hi_ready["1"], 1)
            queries_hi(0, 0)
            queries_hi(0, 1)
            act.wait_ge(scales_ready["b"], 1)
            act.wait_ge(gained["b"], KT)
            for n in ("o", "1", "2"):
                weights_b(n)
            pair(0, mlp=False)
            with act.Fori(0, PAIRS - 2) as i:
                pair(i + 1)
            pair(PAIRS - 1, nxt=False)
            mlp_front(PAIRS - 1)
            gelus(PAIRS - 1, 0, MT)

        @block.vector
        def _(dve):
            def row_stats(n, t, src):
                dve.bn_stats(ln_buf[n]["st"][:, t, :], src).then_inc(ln_step[n], 1)

            def inv_std(n, a, tiles, between=None):
                b = ln_buf[n]
                steps = tiles + 10 + 3 * NEWTON
                at = a * steps
                k = tiles
                between = dict(between or {})

                def results(more):
                    nonlocal k
                    if k - tiles in between:
                        between.pop(k - tiles)()
                    dve.wait_ge(ln_step[n], at + k)
                    k += more

                def vec(x):
                    return b[x][:, :]

                results(3)
                mean_e, mean_o = b["st"][:, :, 1], b["st"][:, :, 4]
                dve.tensor_tensor(vec("b"), mean_e, mean_o, ALU.subtract).then_inc(ln_step[n], 1)
                dve.tensor_tensor(vec("c"), b["st"][:, :, 2], b["st"][:, :, 5], ALU.add).then_inc(ln_step[n], 1)
                dve.tensor_tensor(vec("a"), mean_e, mean_o, ALU.add).then_inc(ln_step[n], 1)
                results(3)
                dve.tensor_tensor(vec("h"), vec("b"), vec("b"), ALU.mult).then_inc(ln_step[n], 1)
                dve.tensor_scalar(vec("y"), vec("c"), 1.0 / E, EPS, ALU.mult, ALU.add).then_inc(ln_step[n], 1)
                dve.tensor_scalar(vec("mean"), vec("a"), 0.5, None, ALU.mult).then_inc(ln_step[n], 1)
                results(1)
                dve.scalar_tensor_tensor(vec("v"), vec("h"), 0.25, vec("y"), ALU.mult, ALU.add)\
                    .then_inc(ln_step[n], 1)
                results(2)
                dve.tensor_scalar(vec("h").bitcast(i32), vec("v").bitcast(i32), 1, None,
                                  ALU.logical_shift_right).then_inc(ln_step[n], 1)
                dve.tensor_scalar(vec("c"), vec("v"), -0.5, None, ALU.mult).then_inc(ln_step[n], 1)
                results(1)
                dve.tensor_scalar(vec("y").bitcast(i32), vec("h").bitcast(i32), -1.0, RSQRT_SEED,
                                  ALU.mult, ALU.add).then_inc(ln_step[n], 1)
                for _ in range(NEWTON):
                    results(1)
                    dve.tensor_tensor(vec("a"), vec("y"), vec("y"), ALU.mult).then_inc(ln_step[n], 1)
                    results(1)
                    dve.tensor_tensor(vec("b"), vec("a"), vec("c"), ALU.mult).then_inc(ln_step[n], 1)
                    results(1)
                    dve.scalar_tensor_tensor(vec("y"), vec("b"), 1.5, vec("y"), ALU.add, ALU.mult)\
                        .then_inc(ln_step[n], 1)
                results(0)
                assert k == steps and not between, (k, steps, between)

            def normalised(n, t, src, hat):
                b = ln_buf[n]
                return dve.tensor_scalar(hat[:, t, :], src, b["mean"][:, t:t + 1], b["y"][:, t:t + 1],
                                         ALU.subtract, ALU.mult)

            def layer_norm(n, src, tiles, hat):
                for t in range(tiles):
                    row_stats(n, t, src(t))
                inv_std(n, 0, tiles)
                for t in range(tiles):
                    ins = normalised(n, t, src(t), hat)
                ins.then_inc(hat_ready[n], 1)

            def lo_part(n, a, src, dst):
                dve.wait_ge(hi_ready[n], a + 1)
                dve.tensor_tensor(dst[:, 1], src[:, :, :], dst[:, 0], ALU.subtract).then_inc(lo_ready[n], 1)

            def gain(n, g, group):
                dve.wait_ge(bias_mm[group], 1)
                for c in range(KT):
                    dve.tensor_scalar(wraw[n][:, c, :], wraw[n][:, c, :], lng[g][:, c:c + 1], None, ALU.mult)\
                        .then_inc(gained[group], 1)

            def magnitude(col, group, src, axis):
                dve.tensor_reduce(amax[group][:, col:col + 1], src, axis, ALU.max, apply_absolute_value=True)\
                    .then_inc(amax_ready[group], 1)

            def scales(group, lo, hi, pairs):
                s, m = scale_step[group], amax_all[group]
                dve.wait_ge(amax_shared[group], 1)
                if group == "a":
                    dve.tensor_tensor(mag[:, 0:3], m[:, 0:3], m[:, 3:6], ALU.max).then_inc(s, 1)
                    k = 1
                else:
                    dve.tensor_tensor(mag[:, 3:4], m[:, 0:1], m[:, 3:4], ALU.max).then_inc(s, 1)
                    dve.tensor_copy(mag[:, 4:6], m[:, 1:3]).then_inc(s, 1)
                    k = 2
                dve.wait_ge(s, k)
                dve.tensor_scalar(pow2[:, lo:hi], mag[:, lo:hi], 1e-30, None, ALU.max).then_inc(s, 1)
                dve.wait_ge(s, k + 1)
                dve.tensor_scalar(inv[:, lo:hi].bitcast(i32), pow2[:, lo:hi].bitcast(i32), 0x7F800000, None,
                                  ALU.bitwise_and).then_inc(s, 1)
                dve.wait_ge(s, k + 2)
                dve.tensor_scalar(scale_dn[:, lo:hi], inv[:, lo:hi], 1.0 / 16, None, ALU.mult).then_inc(s, 1)
                dve.wait_ge(s, k + 3)
                dve.reciprocal(scale_up[:, lo:hi], scale_dn[:, lo:hi]).then_inc(s, 1)
                dve.wait_ge(s, k + 4)

            def weight_lo(n, src):
                dve.wait_ge(whi_ready[n], 1)
                dve.scalar_tensor_tensor(wp[n][:, 1].rearrange("p c n -> p (c n)"),
                                         src.rearrange("p c n -> p (c n)"), scale_up[:, COL[n]:COL[n] + 1],
                                         wp[n][:, 0].rearrange("p c n -> p (c n)"),
                                         ALU.mult, ALU.subtract).then_inc(wlo_ready[n], 1)

            dve.wait_ge(ld_cols, 16)
            dve.tensor_copy(lnb1_rep[:, :, :], lnb[1][:, :, None].broadcast_to([P, KT, P])).then_inc(lnb_rep_ready, 1)
            dve.wait_ge(ld_c[0], 16)
            dve.wait_ge(ld_c[1], 16)
            layer_norm("c", lambda t: c_sb[:, t, :], CTT, c_hat)
            for n in ("k", "v", "q"):
                gain(n, 1, "a")
            dve.wait_ge(gained["a"], 3 * KT)
            for n in ("q", "k", "v"):
                magnitude(COL[n], "a", wraw[n][:, :, :], AX.XY)
            dve.wait_ge(ld_cols, 16)
            dve.tensor_tensor(bfull["q"][:, :], bank[:, 0, 0:KT], bcol["q"][:, :], ALU.add).then_inc(consts_ready, 1)
            dve.tensor_tensor(bfull["k"][:, :], bank[:, 0, KT:2 * KT], bcol["k"][:, :], ALU.add)\
                .then_inc(consts_ready, 1)
            dve.wait_ge(ld_rows, 16)
            dve.tensor_tensor(bv_full[:, :], bank[:, 1, 0:E], brow["v"][:, :], ALU.add).then_inc(consts_ready, 1)
            dve.wait_ge(consts_ready, 4)
            magnitude(3, "a", bfull["q"][:, :], AX.X)
            magnitude(4, "a", bfull["k"][:, :], AX.X)
            magnitude(5, "a", bv_full[:, :], AX.X)
            lo_part("c", 0, c_hat, c_parts)
            dve.wait_ge(pool_const, CONSTS)
            for u in range(2):
                dve.tensor_reduce(evenodd[:, u:u + 1], blocks[:, u:8:2], AX.X, ALU.add).then_inc(consts_ready, 1)
            scales("a", 0, 3, None)
            for n in ("q", "k"):
                dve.tensor_scalar(bscaled[n][:, :], bfull[n][:, :], scale_up[:, COL[n]:COL[n] + 1], None, ALU.mult)
            dve.tensor_scalar(bv_scaled[:, :], bv_full[:, :], scale_up[:, 2:3], None, ALU.mult)
            dve.tensor_tensor(sc_exp0[:, :], scale_dn[:, 0:1], scale_dn[:, 1:2], ALU.mult)\
                .then_inc(scales_ready["a"], 1)
            dve.wait_ge(scales_ready["a"], 1)
            dve.tensor_scalar(sc_exp[:, :], sc_exp0[:, :], float(HD) ** -0.5, None, ALU.mult)\
                .then_inc(scales_ready["a"], 1)
            for n in ("k", "v", "q"):
                weight_lo(n, wraw[n][:, :, :])
            for t in range(CTT):
                dve.wait_ge(cT_hi, t + 1)
                dve.tensor_copy(cT[:, 1, :, t * P:CSTART[t] + P],
                                half16(t % 4)[:, 2 * P:4 * P].rearrange("p (k n) -> p k n", k=KT)
                                [:, :, t * P - CSTART[t]:]).then_inc(cT_lo, 1)
            for h in range(KT):
                for c in range(2):
                    dve.wait_ge(khi_ready, 2 * h + c + 1)
                    dve.scalar_tensor_tensor(k_lo[:, h, c * CCH:(c + 1) * CCH], bank[:, 4 + 2 * h + c, 0:CCH],
                                             bscaled["k"][:, h:h + 1], k_hi[:, h, c * CCH:(c + 1) * CCH],
                                             ALU.add, ALU.subtract).then_inc(klo_ready, 1)
            dve.wait_ge(ld_x[0], 16)
            layer_norm("1", lambda t: x_sb[:, t, :], TT, x_hat)
            for b in range(NBATCH // 2):
                dve.wait_ge(v_mm, b + 1)
                dve.tensor_tensor(v_all[:, 2 * b:2 * b + 2, :], bank[0:SK, b, :].rearrange("p (b n) -> p b n", b=2),
                                  bv_scaled[0:SK, None, :].broadcast_to([SK, 2, E]), ALU.add).then_inc(v_ready, 1)
            lo_part("1", 0, x_hat, x_parts)

            def copy_xT(a):
                for half in range(2):
                    dve.wait_ge(xT_done, 2 * a + half + 1)
                    dve.tensor_copy(xT[:, :, :, half * SQ:(half + 1) * SQ], transposed(half)).then_inc(xT_ready, 1)

            def queries_lo(a, h):
                dve.wait_ge(qhi_ready, a * KT + h + 1)
                dve.scalar_tensor_tensor(q_lo[:, h, :], bank[:, 4 + h, :], bscaled["q"][:, h:h + 1],
                                         q_hi[:, h, :], ALU.add, ALU.subtract).then_inc(qlo_ready, 1)

            def maxima(a, *fills):
                for fill in fills:
                    t, groups = fill // len(FILLS), FILLS[fill % len(FILLS)]
                    dve.wait_ge(s_done, a * NF + fill + 1)
                    s0, s1 = 2 * groups[0], 2 * groups[-1] + 2
                    dve.tensor_reduce(smax[:, t, s0:s1],
                                      bank[:, fill % 4, 0:(s1 - s0) * SK].rearrange("p (h k) -> p h k", k=SK),
                                      AX.X, ALU.max).then_inc(smax_ready, 1)

            def max_scaled(a):
                dve.wait_ge(smax_ready, (a + 1) * NF)
                dve.tensor_scalar(m_parts[:, :, 0, :], smax[:, :, :], -1.0 / SEL, None, ALU.mult)\
                    .then_inc(mhi_ready, 1)
                dve.wait_ge(mhi_ready, a + 1)
                dve.scalar_tensor_tensor(m_parts[:, :, 1, :], smax[:, :, :], -1.0 / SEL, m_parts[:, :, 0, :],
                                         ALU.mult, ALU.subtract).then_inc(m_ready, 1)

            def max_rows(a):
                dve.wait_ge(mT_done, a + 1)
                dve.tensor_copy(mT[96:128, :], half16(4)[0:32, 0:TOK]).then_inc(mT_copied, 1)
                dve.wait_ge(mT_copied, a + 1)
                for g0, g1 in ((0, 2), (2, NG)):
                    dve.tensor_copy(qpack[96:128, g0:g1, :], mT[96:128, None, :].broadcast_to([32, g1 - g0, TOK]))\
                        .then_inc(m_rows, 1)

            def normalise_o(a, t):
                dve.wait_ge(on_done, TT * a + t + 1)
                o_ps = bank[:, t, :].rearrange("p (s d) -> p s d", d=32)
                dve.reciprocal(rden[:, t, :], o_ps[:, :, HD]).then_inc(rden_ready, 1)
                dve.wait_ge(rden_ready, TT * a + t + 1)
                dve.tensor_tensor(o_nat[:, t, :].rearrange("p (s d) -> p s d", d=HD), o_ps[:, :, 0:HD],
                                  rden[:, t, :, None].broadcast_to([P, H, HD]), ALU.mult).then_inc(onat_ready, 1)

            def o_lo(a, t):
                dve.wait_ge(hi_ready["o"], TT * a + t + 1)
                dve.tensor_tensor(o_parts[:, 1, t, :], o_nat[:, t, :], o_parts[:, 0, t, :], ALU.subtract)\
                    .then_inc(lo_ready["o"], 1)

            def back(a, waiting=None, between=None):
                for t in range(TT):
                    normalise_o(a, t)
                    if t:
                        o_lo(a, t - 1)
                o_lo(a, TT - 1)
                if waiting:
                    waiting()
                dve.wait_ge(onT_done, 2 * a + 2)
                dve.tensor_copy(onT[:, :, :, SQ:2 * SQ], transposed(1)).then_inc(onT_second, 1)
                dve.wait_ge(xres_ready, a + 1)
                wait(dve, x1res_ready, a)

                def x1_stats(t):
                    dve.wait_ge(x1_ready, TT * a + t + 1)
                    row_stats("2", t, x1[:, t, :])

                for t in range(TT):
                    dve.wait_ge(wo_done, TT * a + t + 1)
                    dve.scalar_tensor_tensor(x1[:, t, :], bank[:, t, 0:E], sc_vo[:, :], x_res[:, t, :],
                                             ALU.mult, ALU.add).then_inc(x1_ready, 1)
                    if t:
                        x1_stats(t - 1)
                x1_stats(TT - 1)
                inv_std("2", a, TT, between)
                wait(dve, hi_ready["2"], TT * a)
                for t in range(TT):
                    normalised("2", t, x1[:, t, :], y_hat).then_inc(hat_ready["2"], 1)
                    if t:
                        y_lo(a, t - 1)
                y_lo(a, TT - 1)

            def y_lo(a, t):
                dve.wait_ge(hi_ready["2"], TT * a + t + 1)
                dve.tensor_tensor(y_parts[:, 1, t, :], y_hat[:, t, :], y_parts[:, 0, t, :], ALU.subtract)\
                    .then_inc(lo_ready["2"], 1)

            def mlp_front(f):
                dve.wait_ge(yT_done, 2 * f + 2)
                dve.tensor_copy(yT[:, :, :, SQ:2 * SQ], transposed(1)).then_inc(yT_second, 1)

            def gelu_lo(f, m):
                dve.wait_ge(ghi_ready, f * MT + m + 1)
                dve.scalar_tensor_tensor(g_lo[:, m, :], g_full[:, m % 2, :], scale_up[:, 3:4], g_hi[:, m, :],
                                         ALU.mult, ALU.subtract).then_inc(glo_ready, 1)

            def outputs(f, t):
                if t == 0:
                    dve.wait_ge(x1res_ready, f + 1)
                dve.wait_ge(f2_done, f * TT + t + 1)
                dve.scalar_tensor_tensor(x1_res[:, t, :], bank[:, 6 + t % 2, 0:E], sc_12[:, :], x1_res[:, t, :],
                                         ALU.mult, ALU.add).then_inc(out_ready, 1)

            copy_xT(0)
            queries_lo(0, 0)
            queries_lo(0, 1)
            dve.wait_ge(kpack_loaded, 24 * 16)
            dve.wait_ge(consts_ready, 6)
            for u in range(2):
                dve.tensor_scalar(kpack[:, u:H:2, :], kpack[:, u:H:2, :], evenodd[0:96, u:u + 1], None, ALU.mult)\
                    .then_inc(kpack_masked, 1)
            dve.wait_ge(ld_cols, 16)
            gain("1", 2, "b")
            dve.wait_ge(gained["b"], KT)
            magnitude(0, "b", wraw["1"][:, :, :], AX.XY)
            dve.wait_ge(ld_w["o"], 64)
            magnitude(1, "b", wraw["o"][:, :, :], AX.XY)
            dve.wait_ge(ld_w["2"], 16)
            magnitude(2, "b", wraw["2"][:, :, :], AX.XY)
            dve.wait_ge(ld_cols, 16)
            dve.tensor_tensor(bfull["1"][:, :], bank[:, 6, 0:MT], bcol["1"][:, :], ALU.add).then_inc(consts_ready, 1)
            dve.wait_ge(consts_ready, 7)
            magnitude(3, "b", bfull["1"][:, :], AX.X)
            maxima(0, *range(NF))
            max_scaled(0)
            max_rows(0)
            scales("b", 3, 6, None)
            dve.tensor_tensor(sc_vo[:, :], scale_dn[:, 2:3], scale_dn[:, 4:5], ALU.mult)
            dve.tensor_tensor(sc_12[:, :], scale_dn[:, 3:4], scale_dn[:, 5:6], ALU.mult)\
                .then_inc(scales_ready["b"], 1)
            for i in range(1, PAIRS):
                dve.wait_ge(ld_x[i], 16)
            for t in range((PAIRS - 1) * TT):
                row_stats("rest", t, x_sb[:, TT + t, :])
            inv_std("rest", 0, (PAIRS - 1) * TT)
            dve.tensor_copy(ln_buf["rest"]["h"][:, :], ln_buf["rest"]["y"][:, :]).then_inc(rest_ready, 1)
            dve.wait_ge(scales_ready["b"], 1)
            weight_lo("o", wraw["o"][:, :, :])
            copy_xT(1)
            queries_lo(1, 0)
            queries_lo(1, 1)
            for n in ("1", "2"):
                weight_lo(n, wraw[n][:, :, :])
            back(0)

            def pair(a, nxt=True):
                f = a - 1
                mlp_front(f)
                maxima(a, *range(7))
                gelu_lo(f, 0)
                maxima(a, 7, 8)
                gelu_lo(f, 1)
                maxima(a, 9, 10)
                gelu_lo(f, 2)
                maxima(a, 11)
                max_scaled(a)
                gelu_lo(f, 3)
                max_rows(a)
                gelu_lo(f, 4)
                gelu_lo(f, 5)
                gelu_lo(f, 6)
                if nxt:
                    copy_xT(a + 1)
                gelu_lo(f, 7)
                if nxt:
                    queries_lo(a + 1, 0)
                    queries_lo(a + 1, 1)
                outputs(f, 0)
                back(a, lambda: outputs(f, 1), {9: lambda: outputs(f, 2)})
                outputs(f, 3)

            with dve.Fori(0, PAIRS - 2) as i:
                pair(i + 1)
            pair(PAIRS - 1, nxt=False)
            mlp_front(PAIRS - 1)
            for m in range(MT):
                gelu_lo(PAIRS - 1, m)
            for t in range(TT):
                outputs(PAIRS - 1, t)

        @block.tensor
        def _(pe):
            def split_product(dst, lhs, rhs, tiles):
                terms = [(c, a, b) for c in range(tiles) for a, b in ((0, 0), (0, 1), (1, 0))]
                for n, (c, a, b) in enumerate(terms):
                    mm = pe.matmul(dst, lhs(a, c), rhs(b, c), start=(n == 0), stop=(n == len(terms) - 1))
                return mm

            pe.wait_ge(lnb_rep_ready, 1)
            for n in ("k", "v", "q"):
                pe.wait_ge(ld_w[n], 16)
            for j, n in enumerate(("q", "k")):
                for h in range(KT):
                    for c in range(KT):
                        pe.matmul(bank[:, 0, j * KT + h:j * KT + h + 1], wraw[n][:, c, h * P:(h + 1) * P],
                                  lnb[1][:, c:c + 1], start=(c == 0), stop=(c == KT - 1))
            for c in range(KT):
                mm = pe.matmul(bank[:, 1, 0:E], lnb1_rep[:, c, :], wraw["v"][:, c, :],
                               start=(c == 0), stop=(c == KT - 1))
            mm.then_inc(bias_mm["a"], 1)

            pe.wait_ge(pool_const, 4)
            pe.wait_ge(hi_ready["c"], 1)
            pe.wait_ge(lo_ready["c"], 1)
            pe.wait_ge(consts_ready, 4)
            for t in range(CTT):
                if t >= 4:
                    pe.wait_ge(cT_lo, t - 3)
                for part in range(2):
                    for c in range(KT):
                        at = (part * KT + c) * P
                        tr = pe.transpose(half16(t % 4)[:, at:at + P], c_parts[:, part, t, c * P:(c + 1) * P],
                                          ident16[:, :])
                tr.then_inc(cT_done, 1)
            pe.wait_ge(cT_lo, CTT)

            pe.wait_ge(wlo_ready["k"], 1)
            for h in range(KT):
                for c in range(2):
                    split_product(bank[:, 4 + 2 * h + c, 0:CCH],
                                  lambda part, k: wp["k"][:, part, k, h * P:(h + 1) * P],
                                  lambda part, k: cT[:, part, k, c * CCH:(c + 1) * CCH], KT).then_inc(k_mm, 1)
            pe.wait_ge(wlo_ready["v"], 1)
            for b in range(NBATCH):
                mm = split_product(bank[0:SK, b // 2, (b % 2) * E:(b % 2 + 1) * E],
                                   lambda part, k: cT[:, part, k, b * SK:(b + 1) * SK],
                                   lambda part, k: wp["v"][:, part, k, :], KT)
                if b % 2:
                    mm.then_inc(v_mm, 1)

            def transpose_parts(parts, hi, lo, a, tiles, done):
                for t in range(TT):
                    half = t // 2
                    if tiles == TT or t == 0:
                        pe.wait_ge(hi, a * tiles + t % tiles + 1)
                        pe.wait_ge(lo, a * tiles + t % tiles + 1)
                    for part in range(2):
                        for c in range(KT):
                            at = (t % 2) * P
                            tr = pe.transpose(transposed(half)[:, part, c, at:at + P],
                                              parts[:, part, t, c * P:(c + 1) * P], ident16[:, :])
                    if t % 2:
                        tr.then_inc(done, 1)

            def queries(a):
                pe.wait_ge(xT_ready, 2 * a + 2)
                for h in range(KT):
                    split_product(bank[:, 4 + h, :], lambda part, k: wp["q"][:, part, k, h * P:(h + 1) * P],
                                  lambda part, k: xT[:, part, k, :], KT).then_inc(q_done, 1)

            def scores(a, *fills):
                for fill in fills:
                    t, groups = fill // len(FILLS), FILLS[fill % len(FILLS)]
                    kb = t // (TT // 2) * SK
                    if fill == 0:
                        pe.wait_ge(kcur_ready, a + 1)
                        pe.wait_ge(qpack_ready, (a + 1) * 12 * 16)
                        wait(pe, x1_ready, a * TT)
                    if fill >= 4:
                        pe.wait_ge(smax_ready, a * NF + fill - 3)
                    for u, g in enumerate(groups):
                        mm = pe.matmul(bank[:, fill % 4, u * SK2:(u + 1) * SK2], qpack[0:96, g, t * P:(t + 1) * P],
                                       k_cur[0:96, 2 * g:2 * g + 2, kb:kb + SK], start=True, stop=True)
                    mm.then_inc(s_done, 1)

            def max_transposed(a):
                pe.wait_ge(m_ready, a + 1)
                for t in range(TT):
                    tr = pe.transpose(half16(4)[0:32, t * P:(t + 1) * P],
                                      m_parts[:, t, :, :].rearrange("p a h -> p (a h)"), ident16[:, :])
                tr.then_inc(mT_done, 1)

            def scores_t(a, s):
                if s in (0, 2):
                    pe.wait_ge(m_rows, 2 * a + 1 + s // 2)
                if s < 2:
                    pe.wait_ge(smax_ready, (a + 1) * NF)
                else:
                    pe.wait_ge(exp_done, a * NG + s - 1)
                for u in range(2):
                    for b in range(2):
                        mm = pe.matmul(bank[0:SK, 2 * (s % 2) + u, b * SQ:(b + 1) * SQ],
                                       k_cur[:, 2 * s + u, b * SK:(b + 1) * SK], qpack[:, s, b * SQ:(b + 1) * SQ],
                                       start=True, stop=True)
                mm.then_inc(st_done, 1)

            def values(a, g):
                if g == 0:
                    pe.wait_ge(vcur_ready, a + 1)
                if g >= 2:
                    pe.wait_ge(oT_ready, 4 * a + g - 1)
                pe.wait_ge(exp_done, a * NG + 2 * g + 2)
                for b in range(2):
                    for c in range(4):
                        mm = pe.matmul(bank[32 * c:32 * c + 32, 4 + g % 2, b * SQ:(b + 1) * SQ],
                                       v_cur[:, b, head_of(4 * g + c), :], probs[:, 4 * g + c, b * SQ:(b + 1) * SQ],
                                       start=True, stop=True, tile_position=(0, 32 * c), skip_group_check=True)
                mm.then_inc(pv_done, 1)

            def rows_of_outputs(a):
                pe.wait_ge(exp_done, (a + 1) * NG)
                for groups in ((0, 1, 2), (3,)):
                    pe.wait_ge(oT_ready, 4 * a + groups[-1] + 1)
                    for t in range(TT):
                        for g in groups:
                            tr = pe.transpose(bank[:, t, g * P:(g + 1) * P], oT[:, g, t * P:(t + 1) * P],
                                              ident32[:, :])
                        if g == 3:
                            tr.then_inc(on_done, 1)

            def output_projection(a):
                pe.wait_ge(wlo_ready["o"], 1)
                for t in range(TT):
                    if t % 2 == 0:
                        pe.wait_ge((onT_first, onT_second)[t // 2], a + 1)
                    split_product(bank[:, t, 0:E], lambda part, k: onT[:, part, k, t * P:(t + 1) * P],
                                  lambda part, k: wp["o"][:, part, k, :], KT).then_inc(wo_done, 1)

            def mlp_front(f):
                transpose_parts(y_parts, hi_ready["2"], lo_ready["2"], f, TT, yT_done)
                pe.wait_ge(yT_first, f + 1)
                pe.wait_ge(yT_second, f + 1)

            def hidden(f, m):
                if m >= 2:
                    pe.wait_ge(gelu_done, f * MT + m - 1)
                split_product(bank[:, 6 + m % 2, :], lambda part, k: wp["1"][:, part, k, m * P:(m + 1) * P],
                              lambda part, k: yT[:, part, k, :], KT).then_inc(f1_done, 1)

            def mlp_out(f, t):
                if t == 0:
                    pe.wait_ge(gelu_done, f * MT + MT)
                    pe.wait_ge(glo_ready, f * MT + MT)
                if t >= 2:
                    pe.wait_ge(out_ready, f * TT + t - 1)
                split_product(bank[:, 6 + t % 2, 0:E],
                              lambda part, k: (g_hi, g_lo)[part][:, k, t * P:(t + 1) * P],
                              lambda part, k: wp["2"][:, part, k, :], MT).then_inc(f2_done, 1)

            pe.wait_ge(v_ready, NBATCH // 2)
            pe.wait_ge(wlo_ready["q"], 1)
            pe.wait_ge(klo_ready, 2 * KT)
            transpose_parts(x_parts, hi_ready["1"], lo_ready["1"], 0, 1, xT_done)
            queries(0)
            pe.wait_ge(ld_w["1"], 16)
            pe.wait_ge(ld_cols, 16)
            for m in range(MT):
                for c in range(KT):
                    mm = pe.matmul(bank[:, 6, m:m + 1], wraw["1"][:, c, m * P:(m + 1) * P], lnb[2][:, c:c + 1],
                                   start=(c == 0), stop=(c == KT - 1))
            mm.then_inc(bias_mm["b"], 1)

            def pair(a, mlp=True, nxt=True):
                f = a - 1
                if mlp:
                    mlp_front(f)
                    hidden(f, 0)
                scores(a, 4, 5, 6)
                if mlp:
                    hidden(f, 1)
                scores(a, 7, 8, 9)
                if mlp:
                    hidden(f, 2)
                scores(a, 10, 11)
                if mlp:
                    hidden(f, 3)
                    hidden(f, 4)
                max_transposed(a)
                if mlp:
                    hidden(f, 5)
                    hidden(f, 6)
                scores_t(a, 0)
                scores_t(a, 1)
                if mlp:
                    hidden(f, 7)
                if nxt:
                    transpose_parts(x_parts, hi_ready["1"], lo_ready["1"], a + 1, 1, xT_done)
                    queries(a + 1)
                if mlp:
                    mlp_out(f, 0)
                for s in range(2, 6):
                    scores_t(a, s)
                if nxt:
                    pe.wait_ge(qlo_ready, KT * a + 2 * KT)
                values(a, 0)
                scores_t(a, 6)
                scores_t(a, 7)
                for g in range(1, 4):
                    values(a, g)
                rows_of_outputs(a)
                if mlp:
                    mlp_out(f, 1)
                transpose_parts(o_parts, hi_ready["o"], lo_ready["o"], a, TT, onT_done)
                output_projection(a)
                if mlp:
                    mlp_out(f, 2)
                    mlp_out(f, 3)
                if nxt:
                    scores(a + 1, 0, 1, 2, 3)
                if mlp:
                    pe.wait_ge(out_ready, a * TT)

            scores(0, 0, 1, 2, 3)
            pair(0, mlp=False)
            pe.wait_ge(wlo_ready["1"], 1)
            pe.wait_ge(wlo_ready["2"], 1)
            with pe.Fori(0, PAIRS - 2) as i:
                pair(i + 1)
            pair(PAIRS - 1, nxt=False)
            mlp_front(PAIRS - 1)
            for m in range(MT):
                hidden(PAIRS - 1, m)
            for t in range(TT):
                mlp_out(PAIRS - 1, t)


_ORDER = ["x", "ctx_1024"] + ["L0_xattn_" + n for n in ("wq", "wk", "wv", "wo", "w1", "w2")]
_COLUMNS = ["L0_xattn_" + n for n in ("ln1_g", "ln1_b", "ln2_g", "ln2_b", "bq", "bk", "b1")]
_ROWS = ["L0_xattn_" + n for n in ("bv", "bo", "b2")]


def kernel(**inputs):
    import numpy as np
    import concourse.bacc as bacc
    from concourse.bass_utils import run_bass_kernel_spmd

    nc = bacc.Bacc("TRN2", target_bir_lowering=False, num_devices=1)
    arrays, args = {}, []
    laid = {name: np.ascontiguousarray(inputs[name]) for name in _ORDER}
    laid["columns"] = np.ascontiguousarray(np.concatenate([np.asarray(inputs[n]) for n in _COLUMNS]).reshape(-1, 128).T)
    laid["rows"] = np.stack([np.asarray(inputs[n]) for n in _ROWS])
    for name, a in laid.items():
        arrays[f"in_{name}"] = a
        args.append(nc.dram_tensor(f"in_{name}", a.shape, mybir.dt.from_np(a.dtype), kind="ExternalInput").ap())
    out = nc.dram_tensor("out", arrays["in_x"].shape, mybir.dt.float32, kind="ExternalOutput").ap()
    xattn_block_kernel(nc, *args, out)
    r = run_bass_kernel_spmd(nc, [arrays], core_ids=[0])
    return r.results[0]["out"]
```

```python
import concourse.bass as bass
from concourse import mybir
from contextlib import ExitStack



def xattn_block_kernel(nc, x, ctx_in, wq, wk, wv, wo, w1, w2, columns, rows, out):
    f32, f16, i32 = mybir.dt.float32, mybir.dt.float16, mybir.dt.int32
    ALU, ACT, AX = mybir.AluOpType, mybir.ActivationFunctionType, mybir.AxisListType

    NBATCH, SQ, E = x.shape
    SK = ctx_in.shape[1]
    F = w1.shape[1]
    H = 16
    HD = E // H
    P = 128
    KT = E // P
    MT = F // P
    PAIRS = NBATCH // 2
    TOK = 2 * SQ
    TT = TOK // P
    NTOK = NBATCH * SQ
    CTOK = NBATCH * SK
    CSTART = [0, 128, 256, 384, CTOK - P]
    CTT = len(CSTART)
    CCH = CTOK // 2
    SK2 = 2 * SK
    NG = H // 2
    FILLS = [(0, 1, 2), (3, 4, 5), (6, 7)]
    NF = len(FILLS) * TT
    EPS = 1e-5
    SEL = 32768.0
    RSQRT_SEED = float(0x5F3759DF)
    NEWTON = 3
    LN_STEPS = 10 + 3 * NEWTON
    LN_WAITS = (0, 3, 6, 7) + tuple(range(9, LN_STEPS + 1))
    GD = 4
    REST = (PAIRS - 2) * TT
    W1_BIAS = 400
    K_BANKS = (6, 7, 4, 5)
    CONSTS = 13

    def head_of(slot):
        pos = slot // 2
        return 2 * ((pos % 2) * 4 + pos // 2) + slot % 2

    x_t = x.rearrange("b s e -> (b s) e").rearrange("(t p) e -> p t e", p=P)
    out_t = out.rearrange("b s e -> (b s) e").rearrange("(t p) e -> p t e", p=P)
    ctx_rows = ctx_in.rearrange("b s e -> (b s) e")

    stack = ExitStack()
    with stack:
        def sb(name, shape, dt):
            return stack.enter_context(nc.sbuf_tensor(name, shape, dt))

        def sem(name):
            return stack.enter_context(nc.semaphore(name))

        x_sb = sb("x_sb", [P, NTOK // P, E], f32)
        shared = sb("shared", [P, H * TOK], f32)
        shared_g = sb("shared_g", [P, MT * TOK], f32)
        taken = [0]

        def in_shared(dt, words, pattern, **dims):
            view = shared[:, taken[0]:taken[0] + words]
            taken[0] += words
            return (view.bitcast(dt) if dt != f32 else view).rearrange(pattern, **dims)

        c_sb = in_shared(f32, CTT * E, "p (t e) -> p t e", e=E)
        wraw = {n: in_shared(f32, KT * E, "p (c n) -> p c n", n=E) for n in ("q", "k", "v")}
        wraw["o"] = sb("raw_o", [P, KT, E], f32)
        wraw["1"] = shared_g[:, 0:KT * F].rearrange("p (c n) -> p c n", n=F)
        wraw["2"] = shared_g[:, KT * F:KT * F + MT * E].rearrange("p (c n) -> p c n", n=E)
        wp = {n: sb(f"parts_{n}", [P, 2] + list(wraw[n].shape[1:]), f16) for n in wraw}
        cols = sb("cols", [P, 6 * KT + MT], f32)
        lng = {1: cols[:, 0:KT], 2: cols[:, 2 * KT:3 * KT]}
        lnb = {1: cols[:, KT:2 * KT], 2: cols[:, 3 * KT:4 * KT]}
        bcol = {"q": cols[:, 4 * KT:5 * KT], "k": cols[:, 5 * KT:6 * KT], "1": cols[:, 6 * KT:6 * KT + MT]}
        brows = sb("brows", [P, 3, E], f32)
        brow = {n: brows[:, j, :] for j, n in enumerate(("v", "o", "2"))}
        lnb1_rep = in_shared(f32, KT * P, "p (c n) -> p c n", n=P)
        bfull = {n: sb(f"bfull_{n}", [P, MT if n == "1" else KT], f32) for n in bcol}
        bscaled = {n: sb(f"bscaled_{n}", [P, KT], f32) for n in ("q", "k")}
        bv_full = sb("bv_full", [P, E], f32)
        bv_scaled = sb("bv_scaled", [P, E], f32)
        amax = {"a": sb("amax_a", [P, 6], f32), "b": sb("amax_b", [P, 4], f32)}
        amax_all = {"a": sb("amax_all_a", [P, 6], f32), "b": sb("amax_all_b", [P, 4], f32)}
        mag = sb("mag", [P, 6], f32)
        pow2 = sb("pow2", [P, 6], f32)
        inv = sb("inv", [P, 6], f32)
        scale_up = sb("scale_up", [P, 6], f32)
        scale_dn = sb("scale_dn", [P, 6], f32)
        sc_exp0 = sb("sc_exp0", [P, 1], f32)
        sc_exp = sb("sc_exp", [P, 1], f32)
        sc_vo = sb("sc_vo", [P, 1], f32)
        sc_12 = sb("sc_12", [P, 1], f32)
        COL = {"q": 0, "k": 1, "v": 2, "1": 3, "o": 4, "2": 5}

        ident16 = sb("ident16", [P, P], f16)
        ident32 = sb("ident32", [P, P], f32)
        blocks = sb("blocks", [P, 8], f32)
        evenodd = sb("evenodd", [P, 2], f32)
        selector = sb("selector", [P, H], f16)
        zero = sb("zero", [P, 1], f32)

        c_hat = in_shared(f32, CTT * E, "p (t e) -> p t e", e=E)
        c_parts = in_shared(f16, CTT * E, "p (a t e) -> p a t e", a=2, e=E)
        cT = in_shared(f16, KT * CTOK, "p (a k n) -> p a k n", a=2, k=KT)
        k_hi = in_shared(f16, KT * CTOK // 2, "p (k n) -> p k n", k=KT)
        k_lo = in_shared(f16, KT * CTOK // 2, "p (k n) -> p k n", k=KT)
        pack = sb("pack", [P, NG, CTOK], f16)
        kpack = pack[0:96, :, :]
        v_all = sb("v_all", [SK, NBATCH, E], f32)
        k_cur = sb("k_cur", [P, H, SK2], f16)
        v_cur = sb("v_cur", [SK, 2, H, 32], f32)
        x_hat = sb("x_hat", [P, TT, E], f32)
        x_parts = sb("x_parts", [P, 2, TT, E], f16)
        xT = sb("xT", [P, 2, KT, TOK], f16)
        q_hi = sb("q_hi", [P, KT, TOK], f16)
        q_lo = sb("q_lo", [P, KT, TOK], f16)
        qpack = sb("qpack", [P, NG, TOK], f16)
        smax = sb("smax", [P, TT, H], f32)
        m_parts = sb("m_parts", [P, TT, 2, H], f16)
        mT = pack[:, 0, 0:TOK]
        probs = shared[0:SK, :].rearrange("p (h n) -> p h n", h=H)
        oT = sb("oT", [P, 4, TOK], f32)
        rden = sb("rden", [P, TT, H], f32)
        o_nat = sb("o_nat", [P, TT, E], f32)
        o_parts = sb("o_parts", [P, 2, TT, E], f16)
        onT = sb("onT", [P, 2, KT, TOK], f16)
        x_res = sb("x_res", [P, TT, E], f32)
        x1 = sb("x1", [P, TT, E], f32)
        x1_res = sb("x1_res", [P, TT, E], f32)
        y_hat = sb("y_hat", [P, TT, E], f32)
        y_parts = sb("y_parts", [P, 2, TT, E], f16)
        yT = sb("yT", [P, 2, KT, TOK], f16)
        g_full = sb("g_full", [P, GD, TOK], f32)
        g_parts = shared_g[:, :].bitcast(f16).rearrange("p (a m n) -> p a m n", a=2, m=MT)
        g_hi, g_lo = g_parts[:, 0], g_parts[:, 1]
        def ln_buffers(n, w):
            small = {x: sb(f"ln{n}_{x}", [P, w], f32) for x in ("mean", "v", "h", "a", "b", "c", "y")}
            return dict(st=sb(f"ln{n}_st", [P, w, 6], f32), **small)

        ln_buf = {"rest": ln_buffers("rest", REST), "2": ln_buffers("2", TT)}
        for n, w in (("c", CTT), ("1", TT)):
            ln_buf[n] = {x: t[:, 0:w] if x != "st" else t[:, 0:w, :] for x, t in ln_buf["rest"].items()}

        bank = stack.enter_context(nc.psum_tensor("bank", [P, 8, 512], f32))

        def half16(b):
            return bank[:, b, :].bitcast(f16)

        def transposed(half, first=4):
            return half16(first + half).rearrange("p (a k n) -> p a k n", a=2, k=KT)

        ld_c = [sem(f"ld_c{i}") for i in range(2)]
        ld_x = [sem(f"ld_x{i}") for i in range(PAIRS)]
        ld_w = {n: sem(f"ld_w{n}") for n in wraw}
        ld_cols, ld_rows = sem("ld_cols"), sem("ld_rows")
        pool_const = sem("pool_const")
        consts_ready = sem("consts_ready")
        lnb_rep_ready = sem("lnb_rep_ready")
        ln_step = {n: sem(f"ln_step_{n}") for n in ("c", "1", "rest", "2")}
        hat_ready = {n: sem(f"hat_ready_{n}") for n in ("c", "1", "2")}
        hi_ready = {n: sem(f"hi_ready_{n}") for n in ("c", "1", "2", "o")}
        centred = sem("centred")
        lo_ready = {n: sem(f"lo_ready_{n}") for n in ("c", "1", "2", "o")}
        cT_done, cT_hi, cT_lo = sem("cT_done"), sem("cT_hi"), sem("cT_lo")
        bias_mm = {"a": sem("bias_mm_a"), "b": sem("bias_mm_b")}
        gained = {"a": sem("gained_a_ready"), "b": sem("gained_b_ready")}
        amax_ready = {"a": sem("amax_ready_a"), "b": sem("amax_ready_b")}
        amax_shared = {"a": sem("amax_shared_a"), "b": sem("amax_shared_b")}
        scale_step = {"a": sem("scale_step_a"), "b": sem("scale_step_b")}
        scales_ready = {"a": sem("scales_ready_a"), "b": sem("scales_ready_b")}
        whi_ready = {n: sem(f"whi_{n}") for n in wraw}
        wlo_ready = {n: sem(f"wlo_{n}") for n in wraw}
        k_mm, khi_ready, klo_ready = sem("k_mm"), sem("khi_ready"), sem("klo_ready")
        w_scaled = {n: sem(f"scaled_w{n}") for n in ("1", "2")}
        kpack_loaded, kpack_second = sem("kpack_loaded"), sem("kpack_second")
        v_mm, v_copied, v_ready = sem("v_mm"), sem("v_copied"), sem("v_ready")
        kcur_ready, vcur_ready = sem("kcur_ready"), sem("vcur_ready")
        xres_ready, x1res_ready = sem("xres_ready"), sem("x1res_ready")
        xT_done, xT_ready = sem("xT_done"), sem("xT_ready")
        q_done, qhi_ready, qlo_ready = sem("q_done"), sem("qhi_ready"), sem("qlo_ready")
        qpack_ready, q_copied = sem("qpack_ready"), sem("q_copied")
        s_done, smax_ready = sem("s_done"), sem("smax_ready")
        mhi_ready, m_ready, mT_done, mT_copied, m_rows = [sem(n) for n in (
            "mhi_ready", "m_ready", "mT_done", "mT_copied", "m_rows")]
        st_done, exp_done = sem("st_done"), sem("exp_done")
        pv_done, oT_ready = sem("pv_done"), sem("oT_ready")
        on_done, rden_ready, onat_ready = sem("on_done"), sem("rden_ready"), sem("onat_ready")
        onT_done, onT_first, onT_second = sem("onT_done"), sem("onT_first"), sem("onT_second")
        wo_done, x1_ready = sem("wo_done"), sem("x1_ready")
        yT_done, yT_first, yT_second = sem("yT_done"), sem("yT_first"), sem("yT_second")
        f1_done, gelu_done, ghi_ready, glo_ready = [sem(n) for n in ("f1_done", "gelu_done", "ghi_ready", "glo_ready")]
        f2_done, out_ready, out_stored = sem("f2_done"), sem("out_ready"), sem("out_stored")

        block = stack.enter_context(nc.Block())

        def q_packs(pairs):
            return 0 if isinstance(pairs, int) and pairs == 0 else (pairs * 12 - 4) * 16

        def wait(eng, s, value):
            if isinstance(value, int) and value <= 0:
                return
            eng.wait_ge(s, value)

        @block.sync
        def _(sp):
            for i, (lo, hi) in enumerate(((0, 4), (4, 5))):
                src = ctx_rows[0:4 * P, :].rearrange("(t p) e -> p t e", p=P) if i == 0 else \
                    ctx_rows[CTOK - P:CTOK, :].rearrange("(t p) e -> p t e", p=P)
                sp.dma_start(c_sb[:, lo:hi, :], src).then_inc(ld_c[i], 16)
            for n, w in (("k", wk), ("v", wv), ("q", wq)):
                sp.dma_start(wraw[n][:, :, :], w.rearrange("(c p) n -> p c n", p=P)).then_inc(ld_w[n], 16)
            sp.dma_start(x_sb[:, 0:TT, :], x_t[:, 0:TT, :]).then_inc(ld_x[0], 16)
            sp.dma_start(wraw["1"][:, :, :], w1.rearrange("(c p) n -> p c n", p=P)).then_inc(ld_w["1"], 16)
            for hh in range(2):
                for c1 in range(2):
                    src = wo.rearrange("(c k h r) n -> c h r k n", c=2, k=2, h=2)[c1, hh]
                    at = hh * 64 + c1 * 32
                    sp.dma_start(wraw["o"][at:at + 32, :, :], src).then_inc(ld_w["o"], 16)
            sp.dma_start(wraw["2"][:, :, :], w2.rearrange("(c p) n -> p c n", p=P)).then_inc(ld_w["2"], 16)

            for i in range(1, PAIRS):
                sp.dma_start(x_sb[:, i * TT:(i + 1) * TT, :], x_t[:, i * TT:(i + 1) * TT, :]).then_inc(ld_x[i], 16)

            for part, src in ((0, k_hi), (1, k_lo)):
                sp.wait_ge((khi_ready, klo_ready)[part], 2 * KT)
                for j in range(4):
                    role = 2 * part
                    sp.dma_start(kpack[32 * role:32 * role + 32, 2 * j:2 * j + 2, :],
                                 src[32 * j:32 * j + 32, :, :]).then_inc(kpack_loaded, 16)

            def pack_q(a, hi_roles=(0, 2)):
                wait(sp, st_done, a * NG)
                for part, src in ((0, q_hi), (1, q_lo)):
                    sp.wait_ge((qhi_ready, qlo_ready)[part], a * KT + KT)
                    for role in (hi_roles if part == 0 else (1,)):
                        for j in range(4):
                            sp.dma_start(qpack[32 * role:32 * role + 32, 2 * j:2 * j + 2, :],
                                         src[32 * j:32 * j + 32, :, :]).then_inc(qpack_ready, 16)

            def store(f, t0, t1):
                for t in range(t0, t1):
                    sp.wait_ge(out_ready, f * TT + t + 1)
                    sp.dma_start(out_t[:, bass.ds(f * TT + t, 1), :], x1_res[:, t:t + 1, :]).then_inc(out_stored, 16)

            pack_q(0, hi_roles=(0,))
            pack_q(1)
            with sp.Fori(0, PAIRS - 2) as i:
                pack_q(i + 2)
                store(i, 0, TT)
            store(PAIRS - 2, 0, TT)
            store(PAIRS - 1, 0, TT)
            sp.wait_ge(out_stored, 16 * TT * PAIRS)

        @block.gpsimd
        def _(pool):
            made = [0]

            def const_step(ins):
                made[0] += 1
                ins.then_inc(pool_const, 1)
                pool.wait_ge(pool_const, made[0])

            for m in (ident16, ident32):
                const_step(pool.memset(m[:, :], 0.0))
                const_step(pool.affine_select(out=m[:, :], in_=m[:, :], compare_op=ALU.not_equal, fill=1.0, base=0,
                                              pattern=[[-1, P]], channel_multiplier=1))
            const_step(pool.memset(blocks[:, :], 1.0))
            const_step(pool.affine_select(out=blocks[:, :], in_=blocks[:, :], compare_op=ALU.is_ge, fill=0.0,
                                          base=0, pattern=[[-16, 8]], channel_multiplier=1))
            const_step(pool.affine_select(out=blocks[:, :], in_=blocks[:, :], compare_op=ALU.is_ge, fill=0.0,
                                          base=15, pattern=[[16, 8]], channel_multiplier=-1))
            const_step(pool.memset(selector[96:128, :], 0.0))
            for first in (0, 16):
                const_step(pool.affine_select(out=selector[96:128, :], in_=selector[96:128, :],
                                              compare_op=ALU.not_equal, fill=SEL, base=-first,
                                              pattern=[[-1, H]], channel_multiplier=1))
            const_step(pool.memset(zero[:, :], 0.0))
            const_step(pool.memset(v_cur[:, :, :, :], 0.0))
            const_step(pool.memset(v_cur[:, :, :, HD:HD + 1], 1.0))
            def share_magnitudes(g):
                pool.wait_ge(amax_ready[g], 6 if g == "a" else 4)
                pool.partition_all_reduce(amax_all[g][:, :], amax[g][:, :], P,
                                          bass.bass_isa.ReduceOp.max).then_inc(amax_shared[g], 1)
                pool.wait_ge(amax_shared[g], 1)

            def copy_v(a):
                wait(pool, pv_done, a * 4)
                pool.tensor_copy(v_cur[:, :, :, 0:HD],
                                 v_all[:, bass.ds(2 * a, 2), :].rearrange("p b (h d) -> p b h d", h=H))\
                    .then_inc(vcur_ready, 1)
                pool.wait_ge(ld_rows, 16)
                pool.wait_ge(vcur_ready, a + 1)
                wait(pool, x1_ready, a * TT)
                pool.tensor_tensor(x_res[:, :, :], x_sb[:, bass.ds(a * TT, TT), :],
                                   brow["o"][:, None, :].broadcast_to([P, TT, E]), ALU.add).then_inc(xres_ready, 1)
                pool.wait_ge(xres_ready, a + 1)

            def x1_with_bias(a):
                pool.wait_ge(x1_ready, a * TT + TT)
                wait(pool, out_stored, a * TT * 16)
                pool.tensor_tensor(x1_res[:, :, :], x1[:, :, :],
                                   brow["2"][:, None, :].broadcast_to([P, TT, E]), ALU.add).then_inc(x1res_ready, 1)
                pool.wait_ge(x1res_ready, a + 1)

            def normalise_x(a):
                pool.wait_ge(hi_ready["1"], a)
                pool.wait_ge(lo_ready["1"], a)
                pool.tensor_tensor(x_hat[:, :, :], x_sb[:, bass.ds(a * TT, TT), :],
                                   ln_buf["rest"]["mean"][:, bass.ds((a - 2) * TT, TT), None].broadcast_to([P, TT, E]),
                                   ALU.subtract).then_inc(centred, 1)
                pool.wait_ge(centred, a - 1)
                pool.tensor_tensor(x_hat[:, :, :], x_hat[:, :, :],
                                   ln_buf["rest"]["y"][:, bass.ds((a - 2) * TT, TT), None].broadcast_to([P, TT, E]),
                                   ALU.mult).then_inc(hat_ready["1"], 1)
                pool.wait_ge(hat_ready["1"], a + 1)
                pool.wait_ge(xT_done, 2 * a)
                pool.tensor_tensor(x_parts[:, 0], x_hat[:, :, :], zero[:, :, None].broadcast_to([P, TT, E]), ALU.add)\
                    .then_inc(hi_ready["1"], 1)
                pool.wait_ge(hi_ready["1"], a + 1)
                pool.tensor_tensor(x_parts[:, 1], x_hat[:, :, :], x_parts[:, 0], ALU.subtract)\
                    .then_inc(lo_ready["1"], 1)
                pool.wait_ge(lo_ready["1"], a + 1)

            share_magnitudes("a")
            pool.wait_ge(khi_ready, 2 * KT)
            for j in range(4):
                pool.dma_start(kpack[32:64, 2 * j:2 * j + 2, :], k_hi[32 * j:32 * j + 32, :, :])\
                    .then_inc(kpack_second, 16)
            for b in range(NBATCH // 2):
                pool.wait_ge(v_copied, b + 1)
                pool.tensor_tensor(v_all[:, 2 * b:2 * b + 2, :], v_all[:, 2 * b:2 * b + 2, :],
                                   bv_scaled[0:SK, None, :].broadcast_to([SK, 2, E]), ALU.add).then_inc(v_ready, 1)
                pool.wait_ge(v_ready, b + 1)
            pool.wait_ge(ld_rows, 16)
            for i in range(PAIRS):
                pool.wait_ge(ld_x[i], 16)
            copy_v(0)
            share_magnitudes("b")
            for n in ("1", "2"):
                pool.wait_ge(whi_ready[n], 1)
                pool.tensor_tensor(wraw[n][:, :, :], wraw[n][:, :, :],
                                   scale_up[:, COL[n]:COL[n] + 1, None].broadcast_to(list(wraw[n].shape)), ALU.mult)\
                    .then_inc(w_scaled[n], 1)
                pool.wait_ge(w_scaled[n], 1)
                pool.tensor_tensor(wp[n][:, 1], wraw[n][:, :, :], wp[n][:, 0], ALU.subtract)\
                    .then_inc(wlo_ready[n], 1)
            copy_v(1)
            pool.wait_ge(ln_step["rest"], REST + LN_STEPS)
            normalise_x(2)
            x1_with_bias(0)
            copy_v(2)
            with pool.Fori(0, PAIRS - 3) as i:
                normalise_x(i + 3)
                x1_with_bias(i + 1)
                copy_v(i + 3)
            x1_with_bias(PAIRS - 2)
            x1_with_bias(PAIRS - 1)

        @block.scalar
        def _(act):
            def hi_part(n, a, src, dst):
                act.wait_ge(hat_ready[n], a + 1)
                act.activation(dst[:, 0], src[:, :, :], ACT.Copy).then_inc(hi_ready[n], 1)

            act.dma_start(cols[:, :], columns).then_inc(ld_cols, 16)
            act.dma_start(brows[:, :, :], rows.partition_broadcast(P)).then_inc(ld_rows, 16)
            act.wait_ge(pool_const, CONSTS)
            act.activation(k_cur[96:128, :, :], selector[96:128, :, None].broadcast_to([32, H, SK2]),
                           ACT.Copy).then_inc(consts_ready, 1)
            hi_part("c", 0, c_hat, c_parts)
            def context_hi(t):
                act.wait_ge(cT_done, t + 1)
                act.activation(cT[:, 0, :, t * P:CSTART[t] + P],
                               half16(t % 4)[:, 0:2 * P].rearrange("p (k n) -> p k n", k=KT)
                               [:, :, t * P - CSTART[t]:], ACT.Copy)\
                    .then_inc(cT_hi, 1)

            def weight_hi(n):
                act.activation(wp[n][:, 0], wraw[n][:, :, :], ACT.Copy, scale=scale_up[:, COL[n]:COL[n] + 1])\
                    .then_inc(whi_ready[n], 1)

            for t in range(3):
                context_hi(t)
            act.wait_ge(scales_ready["a"], 1)
            act.wait_ge(gained["a"], 3 * KT)
            weight_hi("k")
            for t in range(3, CTT):
                context_hi(t)
            weight_hi("q")
            weight_hi("v")
            for h in range(KT):
                for c in range(2):
                    act.wait_ge(k_mm, 2 * h + c + 1)
                    act.activation(k_hi[:, h, c * CCH:(c + 1) * CCH], bank[:, K_BANKS[2 * h + c], 0:CCH], ACT.Identity,
                                   bias=bscaled["k"][:, h:h + 1]).then_inc(khi_ready, 1)
                    if (h, c) == (0, 1):
                        hi_part("1", 0, x_hat, x_parts)
            act.wait_ge(xT_done, 1)
            act.activation(xT[:, :, :, 0:SQ], transposed(0, 0), ACT.Copy).then_inc(xT_ready, 1)
            act.wait_ge(ld_cols, 16)
            act.wait_ge(bias_mm["b"], 1)
            for c in range(KT):
                act.activation(wraw["1"][:, c, :], wraw["1"][:, c, :], ACT.Copy, scale=lng[2][:, c:c + 1])\
                    .then_inc(gained["b"], 1)

            def queries_hi(a, first=6):
                wait(act, qpack_ready, q_packs(a))
                act.wait_ge(q_done, a * KT + 1)
                act.activation(q_hi[:, 0, :], bank[:, first, :], ACT.Identity, bias=bscaled["q"][:, 0:1])\
                    .then_inc(qhi_ready, 1)

            def exps(a, s0, s1):
                for s in range(s0, s1):
                    act.wait_ge(st_done, a * NG + s + 1)
                    b0 = 2 * (s % 2)
                    act.activation(probs[:, 2 * s:2 * s + 2, :], bank[0:SK, b0:b0 + 2, :], ACT.Exp,
                                   scale=sc_exp[0:SK, :]).then_inc(exp_done, 1)

            def back(a):
                for t in range(TT):
                    act.wait_ge(onat_ready, TT * a + t + 1)
                    act.activation(o_parts[:, 0, t, :], o_nat[:, t, :], ACT.Copy).then_inc(hi_ready["o"], 1)
                act.wait_ge(onT_done, 2 * a + 1)
                act.activation(onT[:, :, :, 0:SQ], transposed(0), ACT.Copy).then_inc(onT_first, 1)

            def split_y(a):
                for t in range(TT):
                    act.wait_ge(hat_ready["2"], TT * a + t + 1)
                    act.activation(y_parts[:, 0, t, :], y_hat[:, t, :], ACT.Copy).then_inc(hi_ready["2"], 1)

            def copy_yT(f):
                act.wait_ge(yT_done, 2 * f + 1)
                act.activation(yT[:, :, :, 0:SQ], transposed(0), ACT.Copy).then_inc(yT_first, 1)

            def gelus(f, m0, m1):
                for m in range(m0, m1):
                    act.wait_ge(f1_done, f * MT + m + 1)
                    if m >= GD:
                        act.wait_ge(glo_ready, f * MT + m - GD + 1)
                    act.activation(g_full[:, m % GD, :], bank[:, 6 + m % 2, :], ACT.Gelu,
                                   bias=bfull["1"][:, m:m + 1], scale=scale_dn[:, 3:4]).then_inc(gelu_done, 1)
                    act.wait_ge(gelu_done, f * MT + m + 1)
                    act.activation(g_hi[:, m, :], g_full[:, m % GD, :], ACT.Copy, scale=scale_up[:, 3:4])\
                        .then_inc(ghi_ready, 1)

            def pair(a, mlp=True, nxt=True):
                if mlp:
                    gelus(a - 1, 0, MT if nxt else 6)
                if mlp:
                    exps(a, 0, NG)
                else:
                    exps(a, 0, 5)
                    queries_hi(a + 1)
                    exps(a, 5, NG)
                    act.wait_ge(scales_ready["b"], 1)
                    weight_hi("o")
                    weight_hi("1")
                if not nxt:
                    gelus(a - 1, 6, MT)
                back(a)
                if not mlp:
                    weight_hi("2")
                split_y(a)
                copy_yT(a)

            queries_hi(0, first=2)
            for b in range(NBATCH // 2):
                act.wait_ge(v_mm, b + 1)
                act.activation(v_all[:, 2 * b:2 * b + 2, :], bank[0:SK, 4 + b, :].rearrange("p (b n) -> p b n", b=2),
                               ACT.Copy).then_inc(v_copied, 1)
            hi_part("1", 1, x_hat, x_parts)
            pair(0, mlp=False)
            with act.Fori(0, PAIRS - 2) as i:
                pair(i + 1)
            pair(PAIRS - 1, nxt=False)
            gelus(PAIRS - 1, 0, MT)

        @block.vector
        def _(dve):
            def row_stats(n, t, src):
                dve.bn_stats(ln_buf[n]["st"][:, t, :], src).then_inc(ln_step[n], 1)

            def inv_std(n, a, tiles, between=None):
                between = dict(between or {})
                for step in inv_std_steps(n, a, tiles):
                    if step in between:
                        between.pop(step)()
                assert not between, between

            def inv_std_steps(n, a, tiles):
                b = ln_buf[n]
                steps = tiles + LN_STEPS
                at = a * steps
                k = tiles

                def results(more):
                    nonlocal k
                    yield k - tiles
                    dve.wait_ge(ln_step[n], at + k)
                    k += more

                def vec(x):
                    return b[x][:, :]

                yield from results(3)
                mean_e, mean_o = b["st"][:, :, 1], b["st"][:, :, 4]
                dve.tensor_tensor(vec("b"), mean_e, mean_o, ALU.subtract).then_inc(ln_step[n], 1)
                dve.tensor_tensor(vec("c"), b["st"][:, :, 2], b["st"][:, :, 5], ALU.add).then_inc(ln_step[n], 1)
                dve.tensor_tensor(vec("a"), mean_e, mean_o, ALU.add).then_inc(ln_step[n], 1)
                yield from results(3)
                dve.tensor_tensor(vec("h"), vec("b"), vec("b"), ALU.mult).then_inc(ln_step[n], 1)
                dve.tensor_scalar(vec("y"), vec("c"), 1.0 / E, EPS, ALU.mult, ALU.add).then_inc(ln_step[n], 1)
                dve.tensor_scalar(vec("mean"), vec("a"), 0.5, None, ALU.mult).then_inc(ln_step[n], 1)
                yield from results(1)
                dve.scalar_tensor_tensor(vec("v"), vec("h"), 0.25, vec("y"), ALU.mult, ALU.add)\
                    .then_inc(ln_step[n], 1)
                yield from results(2)
                dve.tensor_scalar(vec("h").bitcast(i32), vec("v").bitcast(i32), 1, None,
                                  ALU.logical_shift_right).then_inc(ln_step[n], 1)
                dve.tensor_scalar(vec("c"), vec("v"), -0.5, None, ALU.mult).then_inc(ln_step[n], 1)
                yield from results(1)
                dve.tensor_scalar(vec("y").bitcast(i32), vec("h").bitcast(i32), -1.0, RSQRT_SEED,
                                  ALU.mult, ALU.add).then_inc(ln_step[n], 1)
                for _ in range(NEWTON):
                    yield from results(1)
                    dve.tensor_tensor(vec("a"), vec("y"), vec("y"), ALU.mult).then_inc(ln_step[n], 1)
                    yield from results(1)
                    dve.tensor_tensor(vec("b"), vec("a"), vec("c"), ALU.mult).then_inc(ln_step[n], 1)
                    yield from results(1)
                    dve.scalar_tensor_tensor(vec("y"), vec("b"), 1.5, vec("y"), ALU.add, ALU.mult)\
                        .then_inc(ln_step[n], 1)
                yield from results(0)
                assert k == steps, (k, steps)

            def normalised(n, t, src, hat):
                b = ln_buf[n]
                return dve.tensor_scalar(hat[:, t, :], src, b["mean"][:, t:t + 1], b["y"][:, t:t + 1],
                                         ALU.subtract, ALU.mult)

            def all_normalised(n, src, tiles, hat):
                for t in range(tiles):
                    ins = normalised(n, t, src(t), hat)
                ins.then_inc(hat_ready[n], 1)

            def lo_part(n, a, src, dst):
                dve.wait_ge(hi_ready[n], a + 1)
                dve.tensor_tensor(dst[:, 1], src[:, :, :], dst[:, 0], ALU.subtract).then_inc(lo_ready[n], 1)

            def gain(n, products):
                dve.wait_ge(bias_mm["a"], products)
                for c in range(KT):
                    dve.tensor_scalar(wraw[n][:, c, :], wraw[n][:, c, :], lng[1][:, c:c + 1], None, ALU.mult)\
                        .then_inc(gained["a"], 1)

            def magnitude(col, group, src, axis):
                dve.tensor_reduce(amax[group][:, col:col + 1], src, axis, ALU.max, apply_absolute_value=True)\
                    .then_inc(amax_ready[group], 1)

            def scales(group, lo, hi, between=None):
                def results(step):
                    if between:
                        between[step]()
                    dve.wait_ge(s, k + step - 1)

                s, m = scale_step[group], amax_all[group]
                dve.wait_ge(amax_shared[group], 1)
                if group == "a":
                    dve.tensor_tensor(mag[:, 0:3], m[:, 0:3], m[:, 3:6], ALU.max).then_inc(s, 1)
                    k = 1
                else:
                    dve.tensor_tensor(mag[:, 3:4], m[:, 0:1], m[:, 3:4], ALU.max).then_inc(s, 1)
                    dve.tensor_copy(mag[:, 4:6], m[:, 1:3]).then_inc(s, 1)
                    k = 2
                results(1)
                dve.tensor_scalar(pow2[:, lo:hi], mag[:, lo:hi], 1e-30, None, ALU.max).then_inc(s, 1)
                results(2)
                dve.tensor_scalar(inv[:, lo:hi].bitcast(i32), pow2[:, lo:hi].bitcast(i32), 0x7F800000, None,
                                  ALU.bitwise_and).then_inc(s, 1)
                results(3)
                dve.tensor_scalar(scale_dn[:, lo:hi], inv[:, lo:hi], 1.0 / 16, None, ALU.mult).then_inc(s, 1)
                results(4)
                dve.reciprocal(scale_up[:, lo:hi], scale_dn[:, lo:hi]).then_inc(s, 1)
                dve.wait_ge(s, k + 4)

            def weight_lo(n, src):
                dve.wait_ge(whi_ready[n], 1)
                dve.scalar_tensor_tensor(wp[n][:, 1].rearrange("p c n -> p (c n)"),
                                         src.rearrange("p c n -> p (c n)"), scale_up[:, COL[n]:COL[n] + 1],
                                         wp[n][:, 0].rearrange("p c n -> p (c n)"),
                                         ALU.mult, ALU.subtract).then_inc(wlo_ready[n], 1)

            dve.wait_ge(ld_cols, 16)
            dve.tensor_copy(lnb1_rep[:, :, :], lnb[1][:, :, None].broadcast_to([P, KT, P])).then_inc(lnb_rep_ready, 1)
            dve.wait_ge(ld_c[0], 16)
            dve.wait_ge(ld_c[1], 16)
            for t in range(CTT):
                row_stats("c", t, c_sb[:, t, :])
            inv_std("c", 0, CTT, {14: lambda: gain("k", 1)})
            all_normalised("c", lambda t: c_sb[:, t, :], CTT, c_hat)
            gain("v", 2)
            gain("q", 3)
            dve.wait_ge(gained["a"], 3 * KT)
            for n in ("k", "v", "q"):
                magnitude(COL[n], "a", wraw[n][:, :, :], AX.XY)
            dve.tensor_tensor(bfull["q"][:, :], bank[:, 6, 0:KT], bcol["q"][:, :], ALU.add).then_inc(consts_ready, 1)
            dve.tensor_tensor(bfull["k"][:, :], bank[:, 6, KT:2 * KT], bcol["k"][:, :], ALU.add)\
                .then_inc(consts_ready, 1)
            dve.wait_ge(ld_rows, 16)
            dve.tensor_tensor(bv_full[:, :], bank[:, 5, 0:E], brow["v"][:, :], ALU.add).then_inc(consts_ready, 1)
            dve.wait_ge(consts_ready, 4)
            magnitude(3, "a", bfull["q"][:, :], AX.X)
            magnitude(4, "a", bfull["k"][:, :], AX.X)
            magnitude(5, "a", bv_full[:, :], AX.X)
            dve.wait_ge(pool_const, CONSTS)
            for u in range(2):
                dve.tensor_reduce(evenodd[:, u:u + 1], blocks[:, u:8:2], AX.X, ALU.add).then_inc(consts_ready, 1)

            def context_lo(t):
                dve.wait_ge(cT_hi, t + 1)
                dve.tensor_copy(cT[:, 1, :, t * P:CSTART[t] + P],
                                half16(t % 4)[:, 2 * P:4 * P].rearrange("p (k n) -> p k n", k=KT)
                                [:, :, t * P - CSTART[t]:]).then_inc(cT_lo, 1)

            def scales_a():
                def in_gap(step):
                    row_stats("1", step - 1, x_sb[:, step - 1, :])
                    if step > 2:
                        context_lo(step - 3)

                scales("a", 0, 3, {k: (lambda k=k: in_gap(k)) for k in range(1, 5)})
                for n in ("q", "k"):
                    dve.tensor_scalar(bscaled[n][:, :], bfull[n][:, :], scale_up[:, COL[n]:COL[n] + 1], None, ALU.mult)
                dve.tensor_scalar(bv_scaled[:, :], bv_full[:, :], scale_up[:, 2:3], None, ALU.mult)
                dve.tensor_tensor(sc_exp0[:, :], scale_dn[:, 0:1], scale_dn[:, 1:2], ALU.mult)\
                    .then_inc(scales_ready["a"], 1)
                dve.wait_ge(scales_ready["a"], 1)
                dve.tensor_scalar(sc_exp[:, :], sc_exp0[:, :], float(HD) ** -0.5, None, ALU.mult)\
                    .then_inc(scales_ready["a"], 1)

            lo_part("c", 0, c_hat, c_parts)
            dve.wait_ge(ld_x[0], 16)
            scales_a()
            inv_std("1", 0, TT, {0: lambda: context_lo(2), 3: lambda: weight_lo("k", wraw["k"][:, :, :]),
                                 7: lambda: context_lo(3), 10: lambda: context_lo(4)})
            all_normalised("1", lambda t: x_sb[:, t, :], TT, x_hat)

            def keys_lo(kk):
                h, c = kk // 2, kk % 2
                dve.wait_ge(khi_ready, kk + 1)
                dve.scalar_tensor_tensor(k_lo[:, h, c * CCH:(c + 1) * CCH], bank[:, K_BANKS[kk], 0:CCH],
                                         bscaled["k"][:, h:h + 1], k_hi[:, h, c * CCH:(c + 1) * CCH],
                                         ALU.add, ALU.subtract).then_inc(klo_ready, 1)

            keys_lo(0)
            keys_lo(1)
            lo_part("1", 0, x_hat, x_parts)
            weight_lo("q", wraw["q"][:, :, :])

            def copy_xT(a, first=4):
                for half in range(2):
                    dve.wait_ge(xT_done, 2 * a + half + 1)
                    dve.tensor_copy(xT[:, :, :, half * SQ:(half + 1) * SQ], transposed(half, first))\
                        .then_inc(xT_ready, 1)

            def queries_hi(a, first=6, h=1):
                wait(dve, qpack_ready, q_packs(a))
                dve.wait_ge(q_done, a * KT + h + 1)
                dve.tensor_scalar(q_hi[:, h, :], bank[:, first + h, :], bscaled["q"][:, h:h + 1], None, ALU.add)\
                    .then_inc(qhi_ready, 1)

            def queries_lo(a, h, first=6):
                dve.wait_ge(qhi_ready, a * KT + h + 1)
                dve.scalar_tensor_tensor(q_lo[:, h, :], bank[:, first + h, :], bscaled["q"][:, h:h + 1],
                                         q_hi[:, h, :], ALU.add, ALU.subtract).then_inc(qlo_ready, 1)

            def maxima(a, *fills):
                for fill in fills:
                    t, groups = fill // len(FILLS), FILLS[fill % len(FILLS)]
                    dve.wait_ge(s_done, a * NF + fill + 1)
                    s0, s1 = 2 * groups[0], 2 * groups[-1] + 2
                    dve.tensor_reduce(smax[:, t, s0:s1],
                                      bank[:, fill % 4, 0:(s1 - s0) * SK].rearrange("p (h k) -> p h k", k=SK),
                                      AX.X, ALU.max).then_inc(smax_ready, 1)

            def max_scaled(a):
                dve.wait_ge(smax_ready, (a + 1) * NF)
                dve.tensor_scalar(m_parts[:, :, 0, :], smax[:, :, :], -1.0 / SEL, None, ALU.mult)\
                    .then_inc(mhi_ready, 1)
                dve.wait_ge(mhi_ready, a + 1)
                dve.scalar_tensor_tensor(m_parts[:, :, 1, :], smax[:, :, :], -1.0 / SEL, m_parts[:, :, 0, :],
                                         ALU.mult, ALU.subtract).then_inc(m_ready, 1)

            def max_rows(a):
                dve.wait_ge(mT_done, a + 1)
                dve.tensor_copy(mT[96:128, :], half16(4)[0:32, 0:TOK]).then_inc(mT_copied, 1)
                dve.wait_ge(mT_copied, a + 1)
                for g0, g1 in ((0, 2), (2, NG)):
                    dve.tensor_copy(qpack[96:128, g0:g1, :], mT[96:128, None, :].broadcast_to([32, g1 - g0, TOK]))\
                        .then_inc(m_rows, 1)

            def copy_o(a, g):
                dve.wait_ge(pv_done, 4 * a + g + 1)
                dve.tensor_copy(oT[:, g, :], bank[:, 4 + g % 2, :]).then_inc(oT_ready, 1)

            def row_sums(a):
                dve.wait_ge(on_done, TT * a + TT)
                dve.reciprocal(rden[:, :, :], bank[:, 0:TT, :].rearrange("p t (s d) -> p t s d", d=32)[:, :, :, HD])\
                    .then_inc(rden_ready, 1)
                dve.wait_ge(rden_ready, a + 1)

            def normalise_o(a, t):
                dve.tensor_tensor(o_nat[:, t, :].rearrange("p (s d) -> p s d", d=HD),
                                  bank[:, t, :].rearrange("p (s d) -> p s d", d=32)[:, :, 0:HD],
                                  rden[:, t, :, None].broadcast_to([P, H, HD]), ALU.mult).then_inc(onat_ready, 1)

            def o_lo(a, t):
                dve.wait_ge(hi_ready["o"], TT * a + t + 1)
                dve.tensor_tensor(o_parts[:, 1, t, :], o_nat[:, t, :], o_parts[:, 0, t, :], ALU.subtract)\
                    .then_inc(lo_ready["o"], 1)

            def back(a, outputs_0=None, between=None, stats=None, last_gelu=None):
                row_sums(a)
                for t in range(TT):
                    normalise_o(a, t)
                    if t == 0 and last_gelu:
                        last_gelu()
                    if t:
                        o_lo(a, t - 1)
                o_lo(a, TT - 1)
                if outputs_0:
                    outputs_0()
                dve.wait_ge(onT_done, 2 * a + 2)
                dve.tensor_copy(onT[:, :, :, SQ:2 * SQ], transposed(1)).then_inc(onT_second, 1)
                dve.wait_ge(xres_ready, a + 1)
                wait(dve, x1res_ready, a)

                def x1_stats(t):
                    dve.wait_ge(x1_ready, TT * a + t + 1)
                    row_stats("2", t, x1[:, t, :])

                if stats:
                    stats()
                for t in range(TT):
                    dve.wait_ge(wo_done, TT * a + t + 1)
                    dve.scalar_tensor_tensor(x1[:, t, :], bank[:, t, 0:E], sc_vo[:, :], x_res[:, t, :],
                                             ALU.mult, ALU.add).then_inc(x1_ready, 1)
                    if t:
                        x1_stats(t - 1)
                x1_stats(TT - 1)
                inv_std("2", a, TT, between)
                wait(dve, hi_ready["2"], TT * a)
                for t in range(TT):
                    normalised("2", t, x1[:, t, :], y_hat).then_inc(hat_ready["2"], 1)
                    if t:
                        y_lo(a, t - 1)
                y_lo(a, TT - 1)

            def y_lo(a, t):
                dve.wait_ge(hi_ready["2"], TT * a + t + 1)
                dve.tensor_tensor(y_parts[:, 1, t, :], y_hat[:, t, :], y_parts[:, 0, t, :], ALU.subtract)\
                    .then_inc(lo_ready["2"], 1)

            def copy_yT(f):
                dve.wait_ge(yT_done, 2 * f + 2)
                dve.tensor_copy(yT[:, :, :, SQ:2 * SQ], transposed(1)).then_inc(yT_second, 1)

            def gelu_lo(f, m):
                dve.wait_ge(ghi_ready, f * MT + m + 1)
                dve.scalar_tensor_tensor(g_lo[:, m, :], g_full[:, m % GD, :], scale_up[:, 3:4], g_hi[:, m, :],
                                         ALU.mult, ALU.subtract).then_inc(glo_ready, 1)

            def outputs(f, t, first=6):
                if t == 0:
                    dve.wait_ge(x1res_ready, f + 1)
                dve.wait_ge(f2_done, f * TT + t + 1)
                b = first + t % 2 if first else t
                dve.scalar_tensor_tensor(x1_res[:, t, :], bank[:, b, 0:E], sc_12[:, :], x1_res[:, t, :],
                                         ALU.mult, ALU.add).then_inc(out_ready, 1)

            def mask_k(a):
                wait(dve, st_done, a * NG)
                for u in range(2):
                    dve.tensor_scalar(k_cur[0:96, u:H:2, :], kpack[:, :, bass.ds(a * SK2, SK2)],
                                      evenodd[0:96, u:u + 1], None, ALU.mult).then_inc(kcur_ready, 1)

            dve.wait_ge(xT_done, 2)
            dve.tensor_copy(xT[:, :, :, SQ:2 * SQ], transposed(1, 0)).then_inc(xT_ready, 1)
            keys_lo(2)
            keys_lo(3)
            weight_lo("v", wraw["v"][:, :, :])
            dve.wait_ge(bias_mm["b"], 1)
            dve.tensor_tensor(bfull["1"][:, :], bank[:, 7, W1_BIAS:W1_BIAS + MT], bcol["1"][:, :], ALU.add)\
                .then_inc(consts_ready, 1)
            dve.wait_ge(consts_ready, 7)
            magnitude(3, "b", bfull["1"][:, :], AX.X)
            dve.wait_ge(ld_w["o"], 64)
            magnitude(1, "b", wraw["o"][:, :, :], AX.XY)
            queries_lo(0, 0, first=2)
            queries_hi(0, first=2)
            queries_lo(0, 1, first=2)
            for j in range(4):
                dve.wait_ge(qhi_ready, KT)
                dve.tensor_copy(qpack[64:96, 2 * j:2 * j + 2, :], q_hi[32 * j:32 * j + 32, :, :])\
                    .then_inc(q_copied, 1)
            dve.wait_ge(kpack_loaded, 8 * 16)
            dve.wait_ge(kpack_second, 4 * 16)
            mask_k(0)
            dve.wait_ge(ld_x[1], 16)
            for t in range(TT):
                row_stats("1", t, x_sb[:, TT + t, :])
            inv_std("1", 1, TT)
            maxima(0, *range(NF))
            max_scaled(0)
            all_normalised("1", lambda t: x_sb[:, TT + t, :], TT, x_hat)
            max_rows(0)
            lo_part("1", 1, x_hat, x_parts)
            dve.wait_ge(gained["b"], KT)
            magnitude(0, "b", wraw["1"][:, :, :], AX.XY)
            dve.wait_ge(ld_w["2"], 16)
            magnitude(2, "b", wraw["2"][:, :, :], AX.XY)
            copy_xT(1, first=6)
            copy_o(0, 0)
            scales("b", 3, 6)
            dve.tensor_tensor(sc_vo[:, :], scale_dn[:, 2:3], scale_dn[:, 4:5], ALU.mult)
            dve.tensor_tensor(sc_12[:, :], scale_dn[:, 3:4], scale_dn[:, 5:6], ALU.mult)\
                .then_inc(scales_ready["b"], 1)
            queries_lo(1, 0)
            queries_hi(1)
            queries_lo(1, 1)
            copy_o(0, 1)
            mask_k(1)
            for i in range(2, PAIRS):
                dve.wait_ge(ld_x[i], 16)

            def rest_stats(t0, t1):
                for t in range(t0, t1):
                    row_stats("rest", t, x_sb[:, 2 * TT + t, :])

            copy_o(0, 2)
            rest_stats(0, REST // 2)
            copy_o(0, 3)
            dve.wait_ge(scales_ready["b"], 1)
            weight_lo("o", wraw["o"][:, :, :])
            rest = inv_std_steps("rest", 0, REST)
            back(0, stats=lambda: rest_stats(REST // 2, REST), between=dict.fromkeys(LN_WAITS, lambda: next(rest)))
            for _ in rest:
                pass
            copy_yT(0)

            def pair(a, nxt=True):
                f = a - 1
                maxima(a, *range(7))
                gelu_lo(f, 0)
                maxima(a, 7, 8)
                gelu_lo(f, 1)
                maxima(a, 9, 10)
                gelu_lo(f, 2)
                maxima(a, 11)
                max_scaled(a)
                gelu_lo(f, 3)
                max_rows(a)
                gelu_lo(f, 4)
                gelu_lo(f, 5)
                if nxt:
                    copy_xT(a + 1)
                    gelu_lo(f, 6)
                    gelu_lo(f, 7)
                    queries_hi(a + 1, h=0)
                    queries_lo(a + 1, 0)
                    queries_hi(a + 1)
                    queries_lo(a + 1, 1)
                copy_o(a, 0)
                copy_o(a, 1)
                if nxt:
                    mask_k(a + 1)
                copy_o(a, 2)
                copy_o(a, 3)
                if not nxt:
                    gelu_lo(f, 6)
                back(a, lambda: outputs(f, 0), {12: lambda: outputs(f, 1)},
                     last_gelu=None if nxt else lambda: gelu_lo(f, 7))
                outputs(f, 2)
                copy_yT(a)
                outputs(f, 3)

            with dve.Fori(0, PAIRS - 2) as i:
                pair(i + 1)
            pair(PAIRS - 1, nxt=False)
            for m in range(MT):
                gelu_lo(PAIRS - 1, m)
            for t in range(TT):
                outputs(PAIRS - 1, t, first=0)

        @block.tensor
        def _(pe):
            def split_product(dst, lhs, rhs, tiles):
                terms = [(c, a, b) for c in range(tiles) for a, b in ((0, 0), (0, 1), (1, 0))]
                for n, (c, a, b) in enumerate(terms):
                    mm = pe.matmul(dst, lhs(a, c), rhs(b, c), start=(n == 0), stop=(n == len(terms) - 1))
                return mm

            pe.wait_ge(lnb_rep_ready, 1)
            for n in ("k", "v", "q"):
                pe.wait_ge(ld_w[n], 16)
                if n == "v":
                    for c in range(KT):
                        mm = pe.matmul(bank[:, 5, 0:E], lnb1_rep[:, c, :], wraw["v"][:, c, :],
                                       start=(c == 0), stop=(c == KT - 1))
                else:
                    for h in range(KT):
                        for c in range(KT):
                            at = COL[n] * KT + h
                            mm = pe.matmul(bank[:, 6, at:at + 1], wraw[n][:, c, h * P:(h + 1) * P],
                                           lnb[1][:, c:c + 1], start=(c == 0), stop=(c == KT - 1))
                mm.then_inc(bias_mm["a"], 1)

            def w1_bias(m0, m1):
                pe.wait_ge(ld_w["1"], 16)
                pe.wait_ge(ld_cols, 16)
                for m in range(m0, m1):
                    for c in range(KT):
                        mm = pe.matmul(bank[:, 7, W1_BIAS + m:W1_BIAS + m + 1], wraw["1"][:, c, m * P:(m + 1) * P],
                                       lnb[2][:, c:c + 1], start=(c == 0), stop=(c == KT - 1))
                return mm

            w1_bias(0, 6)

            pe.wait_ge(pool_const, 4)
            pe.wait_ge(hi_ready["c"], 1)
            pe.wait_ge(lo_ready["c"], 1)
            for t in range(CTT):
                if t >= 4:
                    pe.wait_ge(cT_lo, t - 3)
                for part in range(2):
                    for c in range(KT):
                        at = (part * KT + c) * P
                        tr = pe.transpose(half16(t % 4)[:, at:at + P], c_parts[:, part, t, c * P:(c + 1) * P],
                                          ident16[:, :])
                tr.then_inc(cT_done, 1)
            w1_bias(6, MT).then_inc(bias_mm["b"], 1)

            def transpose_parts(parts, hi, lo, a, tiles, done, first=4):
                for t in range(TT):
                    half = t // 2
                    if tiles == TT or t == 0:
                        pe.wait_ge(hi, a * tiles + t % tiles + 1)
                        pe.wait_ge(lo, a * tiles + t % tiles + 1)
                    for part in range(2):
                        for c in range(KT):
                            at = (t % 2) * P
                            tr = pe.transpose(transposed(half, first)[:, part, c, at:at + P],
                                              parts[:, part, t, c * P:(c + 1) * P], ident16[:, :])
                    if t % 2:
                        tr.then_inc(done, 1)

            def queries(a, first=6):
                pe.wait_ge(xT_ready, 2 * a + 2)
                for h in range(KT):
                    split_product(bank[:, first + h, :], lambda part, k: wp["q"][:, part, k, h * P:(h + 1) * P],
                                  lambda part, k: xT[:, part, k, :], KT).then_inc(q_done, 1)

            pe.wait_ge(wlo_ready["k"], 1)
            pe.wait_ge(consts_ready, 6)
            for h in range(KT):
                for c in range(2):
                    pe.wait_ge(cT_lo, 3 if (h, c) == (0, 0) else CTT)
                    split_product(bank[:, K_BANKS[2 * h + c], 0:CCH],
                                  lambda part, k: wp["k"][:, part, k, h * P:(h + 1) * P],
                                  lambda part, k: cT[:, part, k, c * CCH:(c + 1) * CCH], KT).then_inc(k_mm, 1)
            transpose_parts(x_parts, hi_ready["1"], lo_ready["1"], 0, 1, xT_done, first=0)
            pe.wait_ge(wlo_ready["q"], 1)
            queries(0, first=2)
            def values_of(batches):
                for b in batches:
                    mm = split_product(bank[0:SK, 4 + b // 2, (b % 2) * E:(b % 2 + 1) * E],
                                       lambda part, k: cT[:, part, k, b * SK:(b + 1) * SK],
                                       lambda part, k: wp["v"][:, part, k, :], KT)
                    if b % 2:
                        mm.then_inc(v_mm, 1)

            pe.wait_ge(klo_ready, 2 * KT)
            pe.wait_ge(wlo_ready["v"], 1)
            pe.wait_ge(consts_ready, 7)
            values_of(range(NBATCH))

            def scores(a, *fills):
                for fill in fills:
                    t, groups = fill // len(FILLS), FILLS[fill % len(FILLS)]
                    kb = t // (TT // 2) * SK
                    if fill == 0:
                        pe.wait_ge(kcur_ready, 2 * a + 2)
                        pe.wait_ge(qpack_ready, q_packs(a + 1))
                        pe.wait_ge(q_copied, 4)
                        wait(pe, x1_ready, a * TT)
                    if fill >= 4:
                        pe.wait_ge(smax_ready, a * NF + fill - 3)
                    for u, g in enumerate(groups):
                        mm = pe.matmul(bank[:, fill % 4, u * SK2:(u + 1) * SK2], qpack[0:96, g, t * P:(t + 1) * P],
                                       k_cur[0:96, 2 * g:2 * g + 2, kb:kb + SK], start=True, stop=True)
                    mm.then_inc(s_done, 1)

            def max_transposed(a):
                pe.wait_ge(m_ready, a + 1)
                for t in range(TT):
                    tr = pe.transpose(half16(4)[0:32, t * P:(t + 1) * P],
                                      m_parts[:, t, :, :].rearrange("p a h -> p (a h)"), ident16[:, :])
                tr.then_inc(mT_done, 1)

            def scores_t(a, s):
                if s in (0, 2):
                    pe.wait_ge(m_rows, 2 * a + 1 + s // 2)
                if s < 2:
                    pe.wait_ge(smax_ready, (a + 1) * NF)
                else:
                    pe.wait_ge(exp_done, a * NG + s - 1)
                for u in range(2):
                    for b in range(2):
                        mm = pe.matmul(bank[0:SK, 2 * (s % 2) + u, b * SQ:(b + 1) * SQ],
                                       k_cur[:, 2 * s + u, b * SK:(b + 1) * SK], qpack[:, s, b * SQ:(b + 1) * SQ],
                                       start=True, stop=True)
                mm.then_inc(st_done, 1)

            def values(a, g):
                if g == 0:
                    pe.wait_ge(vcur_ready, a + 1)
                if g >= 2:
                    pe.wait_ge(oT_ready, 4 * a + g - 1)
                pe.wait_ge(exp_done, a * NG + 2 * g + 2)
                for b in range(2):
                    for c in range(4):
                        mm = pe.matmul(bank[32 * c:32 * c + 32, 4 + g % 2, b * SQ:(b + 1) * SQ],
                                       v_cur[:, b, head_of(4 * g + c), :], probs[:, 4 * g + c, b * SQ:(b + 1) * SQ],
                                       start=True, stop=True, tile_position=(0, 32 * c), skip_group_check=True)
                mm.then_inc(pv_done, 1)

            def rows_of_outputs(a):
                pe.wait_ge(exp_done, (a + 1) * NG)
                for groups in ((0, 1, 2), (3,)):
                    pe.wait_ge(oT_ready, 4 * a + groups[-1] + 1)
                    for t in range(TT):
                        for g in groups:
                            tr = pe.transpose(bank[:, t, g * P:(g + 1) * P], oT[:, g, t * P:(t + 1) * P],
                                              ident32[:, :])
                        if g == 3:
                            tr.then_inc(on_done, 1)

            def output_projection(a):
                pe.wait_ge(wlo_ready["o"], 1)
                for t in range(TT):
                    if t % 2 == 0:
                        pe.wait_ge((onT_first, onT_second)[t // 2], a + 1)
                    split_product(bank[:, t, 0:E], lambda part, k: onT[:, part, k, t * P:(t + 1) * P],
                                  lambda part, k: wp["o"][:, part, k, :], KT).then_inc(wo_done, 1)

            def transpose_y(a):
                transpose_parts(y_parts, hi_ready["2"], lo_ready["2"], a, TT, yT_done)

            def hidden(f, m):
                if m == 0:
                    pe.wait_ge(yT_first, f + 1)
                    pe.wait_ge(yT_second, f + 1)
                if m >= 2:
                    pe.wait_ge(gelu_done, f * MT + m - 1)
                split_product(bank[:, 6 + m % 2, :], lambda part, k: wp["1"][:, part, k, m * P:(m + 1) * P],
                              lambda part, k: yT[:, part, k, :], KT).then_inc(f1_done, 1)

            def mlp_out(f, t, k0=0, k1=MT, first=6):
                if t == 0 and k0 == 0 and first:
                    pe.wait_ge(gelu_done, f * MT + MT - 1)
                if t >= 2 and k0 == 0 and first:
                    pe.wait_ge(out_ready, f * TT + t - 1)
                terms = [(k, part, wpart) for k in range(k0, k1) for part, wpart in ((0, 0), (0, 1), (1, 0))]
                for k, part, wpart in terms:
                    if t == 0 and first and (part, wpart) == (0, 0):
                        pe.wait_ge(glo_ready, f * MT + k + 1)
                    mm = pe.matmul(bank[:, first + (t % 2 if first else t), 0:E],
                                   (g_hi, g_lo)[part][:, k, t * P:(t + 1) * P], wp["2"][:, wpart, k, :],
                                   start=(k == 0 and (part, wpart) == (0, 0)),
                                   stop=(k == MT - 1 and (part, wpart) == (1, 0)))
                if k1 == MT:
                    mm.then_inc(f2_done, 1)

            def pair(a, mlp=True, nxt=True):
                f = a - 1
                if mlp:
                    hidden(f, 0)
                    pe.wait_ge(smax_ready, a * NF + 1)
                scores(a, 4, 5, 6)
                if mlp:
                    hidden(f, 1)
                scores(a, 7, 8, 9)
                if mlp:
                    hidden(f, 2)
                scores(a, 10, 11)
                if mlp:
                    hidden(f, 3)
                    hidden(f, 4)
                    hidden(f, 5)
                else:
                    pe.wait_ge(v_copied, NBATCH // 2)
                max_transposed(a)
                if mlp:
                    hidden(f, 6)
                    if nxt:
                        hidden(f, 7)
                        pe.wait_ge(mT_copied, a + 1)
                        transpose_parts(x_parts, hi_ready["1"], lo_ready["1"], a + 1, 1, xT_done)
                    scores_t(a, 0)
                    scores_t(a, 1)
                    if nxt:
                        pe.wait_ge(gelu_done, f * MT + MT)
                        queries(a + 1)
                    else:
                        hidden(f, 7)
                    scores_t(a, 2)
                    scores_t(a, 3)
                    values(a, 0)
                    scores_t(a, 4)
                    scores_t(a, 5)
                    values(a, 1)
                    scores_t(a, 6)
                    scores_t(a, 7)
                    values(a, 2)
                    values(a, 3)
                else:
                    for s in range(4):
                        scores_t(a, s)
                    transpose_parts(x_parts, hi_ready["1"], lo_ready["1"], a + 1, 1, xT_done, first=6)
                    values(a, 0)
                    scores_t(a, 4)
                    scores_t(a, 5)
                    queries(a + 1)
                    values(a, 1)
                    scores_t(a, 6)
                    scores_t(a, 7)
                    values(a, 2)
                    values(a, 3)
                rows_of_outputs(a)
                if mlp:
                    if nxt:
                        pe.wait_ge(qlo_ready, KT * a + 2 * KT)
                    mlp_out(f, 0)
                transpose_parts(o_parts, hi_ready["o"], lo_ready["o"], a, TT, onT_done)
                output_projection(a)
                if mlp:
                    mlp_out(f, 1)
                    mlp_out(f, 2)
                    mlp_out(f, 3, 0, 5)
                if nxt:
                    scores(a + 1, 0, 1, 2, 3)
                transpose_y(a)
                if mlp:
                    mlp_out(f, 3, 5, MT)

            scores(0, 0, 1, 2, 3)
            pair(0, mlp=False)
            pe.wait_ge(wlo_ready["1"], 1)
            pe.wait_ge(wlo_ready["2"], 1)
            with pe.Fori(0, PAIRS - 2) as i:
                pair(i + 1)
            pair(PAIRS - 1, nxt=False)
            f = PAIRS - 1
            hidden(f, 0)
            pe.wait_ge(out_ready, f * TT)
            hidden(f, 1)
            for m in range(MT):
                if m + 2 < MT:
                    hidden(f, m + 2)
                pe.wait_ge(ghi_ready, f * MT + m + 1)
                pe.wait_ge(glo_ready, f * MT + m + 1)
                for t in range(TT):
                    mlp_out(f, t, m, m + 1, first=0)


_ORDER = ["x", "ctx_1024"] + ["L0_xattn_" + n for n in ("wq", "wk", "wv", "wo", "w1", "w2")]
_COLUMNS = ["L0_xattn_" + n for n in ("ln1_g", "ln1_b", "ln2_g", "ln2_b", "bq", "bk", "b1")]
_ROWS = ["L0_xattn_" + n for n in ("bv", "bo", "b2")]


def kernel(**inputs):
    import numpy as np
    import concourse.bacc as bacc
    from concourse.bass_utils import run_bass_kernel_spmd

    nc = bacc.Bacc("TRN2", target_bir_lowering=False, num_devices=1)
    arrays, args = {}, []
    laid = {name: np.ascontiguousarray(inputs[name]) for name in _ORDER}
    laid["columns"] = np.ascontiguousarray(np.concatenate([np.asarray(inputs[n]) for n in _COLUMNS]).reshape(-1, 128).T)
    laid["rows"] = np.stack([np.asarray(inputs[n]) for n in _ROWS])
    for name, a in laid.items():
        arrays[f"in_{name}"] = a
        args.append(nc.dram_tensor(f"in_{name}", a.shape, mybir.dt.from_np(a.dtype), kind="ExternalInput").ap())
    out = nc.dram_tensor("out", arrays["in_x"].shape, mybir.dt.float32, kind="ExternalOutput").ap()
    xattn_block_kernel(nc, *args, out)
    r = run_bass_kernel_spmd(nc, [arrays], core_ids=[0])
    return r.results[0]["out"]
```
